# Optimizing a Trainium2 kernel written in Bass

```python
import numpy as np
import jax
import jax.numpy as jnp

def _softmax(x, axis=-1):
    return jax.nn.softmax(x, axis=axis)

def _gelu(x):
    return jax.nn.gelu(x, approximate=True)

def _silu(x):
    return jax.nn.silu(x)

def _sigmoid(x):
    return jax.nn.sigmoid(x)

def _layernorm(x, axis=-1, eps=1e-05):
    m = jnp.mean(x, axis=axis, keepdims=True)
    v = jnp.var(x, axis=axis, keepdims=True)
    return (x - m) / jnp.sqrt(v + eps)

def _scatter_add(tgt, idx, src, axis=0):
    return tgt.at[idx].add(src)

def _segment_sum(src, seg, n):
    return jax.ops.segment_sum(src, seg, n)
kernel_name = 'mk_conv_preact_d2_conv_nchw512_r4_e65bf3'

def setup_inputs(seed: int=0):
    np.random.seed(seed)
    _w = jnp.asarray

    def _rec_inputs():
        import jax
        import jax.numpy as jnp
        _gk = jax.random.key(seed)
        x = -8.268e-05 + 0.9999 * jax.random.normal(jax.random.fold_in(_gk, 1), (32, 128, 56, 56), jnp.float32)
        return x
    x = _rec_inputs()

    def _L0_conv_setup():
        import jax, jax.numpy as jnp
        import numpy as np
        from jax import lax
        key = jax.random.key(seed)
        k1, k2, k3 = jax.random.split(key, 3)
        B, C, H, W = (32, 128, 56, 56)
        K = 3
        x = jax.random.normal(k1, (B, C, H, W), dtype=jnp.float32)
        w_offset = jax.random.normal(k2, (K, 1, K), dtype=jnp.float32) * 0.1
        w_deform = jax.random.normal(k3, (1, 1, K), dtype=jnp.float32) * 0.5
        b_deform = jnp.zeros((1,), dtype=jnp.float32)
        return {'x': x, 'w_offset': w_offset, 'w_deform': w_deform, 'b_deform': b_deform}
    _L0_conv_all = _L0_conv_setup()
    _L0_conv_in = {k: v for k, v in _L0_conv_all.items() if k in ('w_offset', 'w_deform', 'b_deform')}
    del _L0_conv_all

    def _L1_conv_setup():
        import jax, jax.numpy as jnp
        import numpy as np
        KS = 3
        DILS = (1, 2, 4)
        EPS = 1e-05

        def _unfold3(x, d):
            b, c, h, w = x.shape
            xp = jnp.pad(x, ((0, 0), (0, 0), (d, d), (d, d)))
            pats = [xp[:, :, i * d:i * d + h, j * d:j * d + w] for i in range(KS) for j in range(KS)]
            return jnp.stack(pats, axis=2)

        def _conv1x1(x, w, b):
            return jnp.einsum('bchw,oc->bohw', x, w) + b[None, :, None, None]

        def _bn_relu(x, g, be, m, v):
            s = g / jnp.sqrt(v + EPS)
            return jax.nn.relu(x * s[None, :, None, None] + (be - m * s)[None, :, None, None])

        def _proj(x, w1, b1, g1, be1, m1, v1, w2, b2, g2, be2, m2, v2):
            h = _bn_relu(_conv1x1(x, w1, b1), g1, be1, m1, v1)
            return _bn_relu(_conv1x1(h, w2, b2), g2, be2, m2, v2)
        key = jax.random.key(seed)
        Cin, Ck, Cv, Cout = (128, 64, 64, 128)
        B, H, W = (4, 16, 16)
        ks = iter(jax.random.split(key, 48))

        def nrm(shape, s=0.02):
            return jax.random.normal(next(ks), shape, jnp.float32) * s

        def bn(c):
            return (jnp.ones((c,), jnp.float32) + nrm((c,), 0.1), nrm((c,), 0.1), nrm((c,), 0.1), jax.random.uniform(next(ks), (c,), jnp.float32, 0.5, 1.5))
        inp = {'x': jax.random.normal(next(ks), (B, Cin, H, W), jnp.float32)}
        for p in ('k', 'q'):
            g1, be1, m1, v1 = bn(Ck)
            g2, be2, m2, v2 = bn(Ck)
            inp.update({p + '1_w': nrm((Ck, Cin)), p + '1_b': nrm((Ck,)), p + '1_g': g1, p + '1_be': be1, p + '1_m': m1, p + '1_v': v1, p + '2_w': nrm((Ck, Ck)), p + '2_b': nrm((Ck,)), p + '2_g': g2, p + '2_be': be2, p + '2_m': m2, p + '2_v': v2})
        inp['v_w'] = nrm((Cv, Cin))
        inp['v_b'] = nrm((Cv,))
        inp['w_w'] = nrm((Cout, Cv))
        inp['w_b'] = nrm((Cout,))
        return inp
    _L1_conv_all = _L1_conv_setup()
    _L1_conv_in = {k: v for k, v in _L1_conv_all.items() if k in ('k1_w', 'k1_b', 'k1_g', 'k1_be', 'k1_m', 'k1_v', 'k2_w', 'k2_b', 'k2_g', 'k2_be', 'k2_m', 'k2_v', 'q1_w', 'q1_b', 'q1_g', 'q1_be', 'q1_m', 'q1_v', 'q2_w', 'q2_b', 'q2_g', 'q2_be', 'q2_m', 'q2_v', 'v_w', 'v_b', 'w_w', 'w_b')}
    del _L1_conv_all
    return {'x': x, 'L0_conv_w_offset': _L0_conv_in['w_offset'], 'L0_conv_w_deform': _L0_conv_in['w_deform'], 'L0_conv_b_deform': _L0_conv_in['b_deform'], 'L1_conv_k1_w': _L1_conv_in['k1_w'], 'L1_conv_k1_b': _L1_conv_in['k1_b'], 'L1_conv_k1_g': _L1_conv_in['k1_g'], 'L1_conv_k1_be': _L1_conv_in['k1_be'], 'L1_conv_k1_m': _L1_conv_in['k1_m'], 'L1_conv_k1_v': _L1_conv_in['k1_v'], 'L1_conv_k2_w': _L1_conv_in['k2_w'], 'L1_conv_k2_b': _L1_conv_in['k2_b'], 'L1_conv_k2_g': _L1_conv_in['k2_g'], 'L1_conv_k2_be': _L1_conv_in['k2_be'], 'L1_conv_k2_m': _L1_conv_in['k2_m'], 'L1_conv_k2_v': _L1_conv_in['k2_v'], 'L1_conv_q1_w': _L1_conv_in['q1_w'], 'L1_conv_q1_b': _L1_conv_in['q1_b'], 'L1_conv_q1_g': _L1_conv_in['q1_g'], 'L1_conv_q1_be': _L1_conv_in['q1_be'], 'L1_conv_q1_m': _L1_conv_in['q1_m'], 'L1_conv_q1_v': _L1_conv_in['q1_v'], 'L1_conv_q2_w': _L1_conv_in['q2_w'], 'L1_conv_q2_b': _L1_conv_in['q2_b'], 'L1_conv_q2_g': _L1_conv_in['q2_g'], 'L1_conv_q2_be': _L1_conv_in['q2_be'], 'L1_conv_q2_m': _L1_conv_in['q2_m'], 'L1_conv_q2_v': _L1_conv_in['q2_v'], 'L1_conv_v_w': _L1_conv_in['v_w'], 'L1_conv_v_b': _L1_conv_in['v_b'], 'L1_conv_w_w': _L1_conv_in['w_w'], 'L1_conv_w_b': _L1_conv_in['w_b']}

def reference(x, L0_conv_w_offset, L0_conv_w_deform, L0_conv_b_deform, L1_conv_k1_w, L1_conv_k1_b, L1_conv_k1_g, L1_conv_k1_be, L1_conv_k1_m, L1_conv_k1_v, L1_conv_k2_w, L1_conv_k2_b, L1_conv_k2_g, L1_conv_k2_be, L1_conv_k2_m, L1_conv_k2_v, L1_conv_q1_w, L1_conv_q1_b, L1_conv_q1_g, L1_conv_q1_be, L1_conv_q1_m, L1_conv_q1_v, L1_conv_q2_w, L1_conv_q2_b, L1_conv_q2_g, L1_conv_q2_be, L1_conv_q2_m, L1_conv_q2_v, L1_conv_v_w, L1_conv_v_b, L1_conv_w_w, L1_conv_w_b):
    import jax
    import jax.numpy as jnp

    def _L0_conv_ref(x, w_offset, w_deform, b_deform):
        import jax, jax.numpy as jnp
        import numpy as np
        from jax import lax
        B, C, H, W = x.shape
        K = w_offset.shape[0]
        pad = (K - 1) // 2
        pooled = jnp.mean(x, axis=(2, 3))
        seq = pooled[:, None, :]
        offset = lax.conv_general_dilated(seq, w_offset, window_strides=(1,), padding=[(pad, pad)], dimension_numbers=('NCH', 'OIH', 'NCH'))
        i_idx = jnp.arange(C, dtype=jnp.float32)
        k_idx = jnp.arange(K, dtype=jnp.float32)
        base = i_idx[None, :] + k_idx[:, None] - pad
        p = jnp.clip(base[None] + offset, 0.0, C - 1.0)
        p0 = jnp.floor(p)
        frac = p - p0
        idx0 = p0.astype(jnp.int32)
        idx1 = jnp.minimum(idx0 + 1, C - 1)
        pooled_b = pooled[:, None, :]
        g0 = jnp.take_along_axis(jnp.broadcast_to(pooled_b, p.shape), idx0, axis=2)
        g1 = jnp.take_along_axis(jnp.broadcast_to(pooled_b, p.shape), idx1, axis=2)
        samp = g0 * (1.0 - frac) + g1 * frac
        out = jnp.einsum('bkc,k->bc', samp, w_deform[0, 0]) + b_deform[0]
        gate = jax.nn.sigmoid(out)[:, :, None, None]
        return x * gate

    def _L1_conv_ref(x, k1_w, k1_b, k1_g, k1_be, k1_m, k1_v, k2_w, k2_b, k2_g, k2_be, k2_m, k2_v, q1_w, q1_b, q1_g, q1_be, q1_m, q1_v, q2_w, q2_b, q2_g, q2_be, q2_m, q2_v, v_w, v_b, w_w, w_b):
        import jax, jax.numpy as jnp
        import numpy as np
        KS = 3
        DILS = (1, 2, 4)
        EPS = 1e-05

        def _unfold3(x, d):
            b, c, h, w = x.shape
            xp = jnp.pad(x, ((0, 0), (0, 0), (d, d), (d, d)))
            pats = [xp[:, :, i * d:i * d + h, j * d:j * d + w] for i in range(KS) for j in range(KS)]
            return jnp.stack(pats, axis=2)

        def _conv1x1(x, w, b):
            return jnp.einsum('bchw,oc->bohw', x, w) + b[None, :, None, None]

        def _bn_relu(x, g, be, m, v):
            s = g / jnp.sqrt(v + EPS)
            return jax.nn.relu(x * s[None, :, None, None] + (be - m * s)[None, :, None, None])

        def _proj(x, w1, b1, g1, be1, m1, v1, w2, b2, g2, be2, m2, v2):
            h = _bn_relu(_conv1x1(x, w1, b1), g1, be1, m1, v1)
            return _bn_relu(_conv1x1(h, w2, b2), g2, be2, m2, v2)
        value = _conv1x1(x, v_w, v_b)
        keyf = _proj(x, k1_w, k1_b, k1_g, k1_be, k1_m, k1_v, k2_w, k2_b, k2_g, k2_be, k2_m, k2_v)
        query = _proj(x, q1_w, q1_b, q1_g, q1_be, q1_m, q1_v, q2_w, q2_b, q2_g, q2_be, q2_m, q2_v)
        uk = jnp.concatenate([_unfold3(keyf, d) for d in DILS], axis=2)
        uv = jnp.concatenate([_unfold3(value, d) for d in DILS], axis=2)
        sim = jnp.sum(uk * query[:, :, None], axis=1, keepdims=True)
        sim = jax.nn.softmax(sim, axis=2)
        context = jnp.sum(sim * uv, axis=2)
        return _conv1x1(context, w_w, w_b)

    def _gn(v, G=32, eps=1e-05):
        B_, C_, H_, W_ = v.shape
        g = v.reshape(B_, G, C_ // G, H_, W_)
        m = jnp.mean(g, axis=(2, 3, 4), keepdims=True)
        s = jnp.var(g, axis=(2, 3, 4), keepdims=True)
        return ((g - m) / jnp.sqrt(s + eps)).reshape(v.shape)

    def _ln_c(v, eps=1e-06):
        m = jnp.mean(v, axis=1, keepdims=True)
        s = jnp.var(v, axis=1, keepdims=True)
        return (v - m) / jnp.sqrt(s + eps)

    def _ln_t(v, eps=1e-05):
        m = jnp.mean(v, axis=-1, keepdims=True)
        s = jnp.var(v, axis=-1, keepdims=True)
        return (v - m) / jnp.sqrt(s + eps)

    def _to_tokens(v):
        B_, C_, H_, W_ = v.shape
        return v.reshape(B_, C_, H_ * W_).transpose(0, 2, 1)

    def _from_tokens(t, like):
        B_, C_, H_, W_ = like.shape
        return t.transpose(0, 2, 1).reshape(B_, C_, H_, W_)
    x = x + _L0_conv_ref(_gn(x), L0_conv_w_offset, L0_conv_w_deform, L0_conv_b_deform)
    x = x + _L1_conv_ref(_gn(x), L1_conv_k1_w, L1_conv_k1_b, L1_conv_k1_g, L1_conv_k1_be, L1_conv_k1_m, L1_conv_k1_v, L1_conv_k2_w, L1_conv_k2_b, L1_conv_k2_g, L1_conv_k2_be, L1_conv_k2_m, L1_conv_k2_v, L1_conv_q1_w, L1_conv_q1_b, L1_conv_q1_g, L1_conv_q1_be, L1_conv_q1_m, L1_conv_q1_v, L1_conv_q2_w, L1_conv_q2_b, L1_conv_q2_g, L1_conv_q2_be, L1_conv_q2_m, L1_conv_q2_v, L1_conv_v_w, L1_conv_v_b, L1_conv_w_w, L1_conv_w_b)
    return x

_drawn_inputs = setup_inputs


def setup_inputs(seed=0):
    import zlib

    import numpy as np

    out = dict(_drawn_inputs(seed))
    spreads = {}
    factors = {'L0_conv_w_offset': 32.891,
     'L0_conv_w_deform': 8.0,
     'L1_conv_k1_w': 8.0,
     'L1_conv_k1_b': 8.0,
     'L1_conv_k1_g': 8.0,
     'L1_conv_k1_be': 8.0,
     'L1_conv_k1_m': 8.0,
     'L1_conv_k1_v': 8.0,
     'L1_conv_k2_w': 8.0,
     'L1_conv_k2_b': 8.0,
     'L1_conv_k2_g': 8.0,
     'L1_conv_k2_be': 8.0,
     'L1_conv_k2_m': 8.0,
     'L1_conv_k2_v': 8.0,
     'L1_conv_q1_w': 8.0,
     'L1_conv_q1_b': 8.0,
     'L1_conv_q1_g': 8.0,
     'L1_conv_q1_be': 8.0,
     'L1_conv_q1_m': 8.0,
     'L1_conv_q1_v': 8.0,
     'L1_conv_q2_w': 8.0,
     'L1_conv_q2_b': 8.0,
     'L1_conv_q2_g': 8.0,
     'L1_conv_q2_be': 8.0,
     'L1_conv_q2_m': 8.0,
     'L1_conv_q2_v': 8.0,
     'L1_conv_v_w': 8.0,
     'L1_conv_v_b': 8.0,
     'L1_conv_w_w': 8.0,
     'L1_conv_w_b': 4.268}
    for name, (base, spread) in spreads.items():
        noise = np.random.default_rng([zlib.crc32(name.encode()), seed]).standard_normal(out[name].shape)
        drawn = base * np.exp(spread * noise) if base else spread * noise
        out[name] = jnp.asarray(drawn.astype(out[name].dtype))
    for name, factor in factors.items():
        out[name] = (out[name] * factor).astype(out[name].dtype)
    return out
```

```python
from contextlib import ExitStack

import concourse.bass as bass
from concourse import mybir

F32 = mybir.dt.float32
F32R = mybir.dt.float32r
I32 = mybir.dt.int32
ALU = mybir.AluOpType
ACT = mybir.ActivationFunctionType

P = 128
NIMG = 32
PAIR = 2
ROUNDS = (NIMG - 4) // PAIR
H = W = 56
HALO = 4
HD = 64
UROWS = 8
UNITS = H // UROWS
UPIX = UROWS * W
PROWS = H + 2 * HALO
PCOLS = W + 2 * HALO
KCOLS = PCOLS + 2
SW = 7
STRIPS = W // SW
WIN = SW + 2 * HALO
WINE = WIN + 1
CROWS = 8
CHUNKS = PROWS // CROWS
CKEYS = CROWS * WIN
VCOLS = HD + 1
TILES = 4 * STRIPS
TPG = 4
GROUPS = TILES // TPG
MAXQ = 16 * SW
GN = 4
EPS = 1e-5
NEG = -1e30
LN3 = 1.0986122886681098
TAPS = 3


def tile(k):
    band, strip = divmod(k, STRIPS)
    rows = min(16, H - 16 * band)
    return band, strip, rows, rows * SW


def window_chunks(k):
    band, _, rows, _ = tile(k)
    return range(2 * band, 2 * band + (rows + 2 * HALO) // CROWS)


YW_PARTS = ((slice(1, STRIPS - 1), slice(0, WIN)), (slice(0, 1), slice(HALO, WIN)),
            (slice(STRIPS - 1, STRIPS), slice(0, WIN - HALO)))

Y_SLOT = [-20, -16, -12, -8, -4, 0, 5]
BAND_UNITS = [3, 5, 7, 7]
BAND_CHUNKS = [3, 5, 7, 8]
CH = dict(stats=13, aggr=20, c1=21, d1=22, c2=23, d3=24, c3=27, d4=28, d6=34, d7=35, c4=37, d9=38,
          c5=39, d11=40)
N_DG, N_PG, N_CG, N_AG = 12, 37, 5, 4


class Image:

    def __init__(self, offset, register=None):
        self.offset, self.register = offset, register

    def __add__(self, n):
        return Image(self.offset + n, self.register)

    def exists(self):
        return self.register is not None or 0 <= self.offset < NIMG

    def parity(self):
        return self.offset % 2

    def index(self):
        return self.offset if self.register is None else self.register * PAIR + self.offset


class Event:

    def __init__(self, sem, per, step=1):
        self.sem, self.per, self.step = sem, per, step
        self.before, self.here = 0, 0

    def next(self, n=1):
        self.here += n
        return self.sem

    def count(self, m, k):
        return max(0, m.offset // self.step * self.per + k - self.before)

    def end_part(self, rounds):
        self.before += self.here * rounds
        self.here = 0


def lagged(n, t, lag):
    return (n, t - lag) if t >= lag else (n + -1, t - lag + TILES)


def slots(first, last, drain=0, register=None):
    for o in range(first, last + 1):
        for t in range(TILES):
            yield Image(o, register), t
    for t in range(drain):
        yield Image(last + 1, register), t


def build(nc, x, par, w1, w2, wv, wo, bo, bv, wg, out):
    x_d = x.rearrange("n c p -> n c p")
    with ExitStack() as ctx:
        def sb(name, shape, dt=F32):
            return ctx.enter_context(nc.sbuf_tensor(name, shape, dt))

        def sem(name):
            return ctx.enter_context(nc.semaphore(name))

        ident = sb("ident", [P, P])
        ones = sb("ones", [P, P])
        group_avg = sb("group_avg", [P, P])
        band = sb("band", [P, TAPS, P])
        conv = sb("conv", [P, TAPS, P])
        iota_i = sb("iota_i", [P, P], I32)
        iota_f = sb("iota_f", [P, P])
        base_i = sb("base_i", [P, TAPS], I32)
        base_f = sb("base_f", [P, TAPS])
        mhalf = sb("mhalf", [P, TAPS])
        mask = sb("mask", [P, 3 * CROWS, WIN])
        vbias = sb("vbias", [P, 3, STRIPS, HD])
        par_s = sb("par_s", [P, 3, 5])
        bn_s = sb("bn_s", [P, 3])
        bn_t = sb("bn_t", [P, 3])
        bn_w = sb("bn_w", [P, 4, 3])
        w1_s = sb("w1_s", [P, P])
        w2_s = sb("w2_s", [P, P])
        wv_s = sb("wv_s", [HD, P])
        wo_s = sb("wo_s", [P, P])
        bo_s = sb("bo_s", [P, 1])
        bv_s = sb("bv_s", [1, HD])
        wg_s = sb("wg_s", [P, 13])
        nbd = sb("nbd", [P, 1])
        w1T = sb("w1T", [P, P])
        w2T = sb("w2T", [P, P])
        wvT = sb("wvT", [P, HD])
        woT = sb("woT", [P, 2, P])
        raw = sb("raw", [P, 2, H * W])
        x1 = sb("x1", [P, H, W])
        y = sb("y", [P, 2, UPIX])
        yw = sb("yw", [P, 4, STRIPS, CKEYS])
        hid = sb("hid", [P, UROWS, W])
        tq = sb("tq", [P, UROWS, W])
        tk = sb("tk", [P, UROWS, W])
        qq = sb("qq", [P, TILES, MAXQ], F32R)
        kh = sb("kh", [P, PROWS, KCOLS], F32R)
        kl = sb("kl", [HD, PROWS, KCOLS], F32R)
        v = sb("v", [CKEYS, CHUNKS, STRIPS, VCOLS])
        z = sb("z", [MAXQ, 2, 3 * CROWS * WIN])
        zmin = sb("zmin", [MAXQ, 2])
        e = sb("e", [MAXQ, 2, 3 * CROWS * WIN])
        eT = sb("eT", [CKEYS, 2, 3 * MAXQ])
        rden = sb("rden", [MAXQ, TPG])
        cx = sb("cx", [MAXQ, TPG, HD])
        cT = sb("cT", [P, 2, MAXQ])
        ost = sb("ost", [P, 2, 16, W])
        stats = sb("stats", [P, UNITS, 6])
        st = sb("st", [P, 2])
        g1 = sb("g1", [P, 48])
        hats = sb("hats", [P, TAPS, 2, P])
        hat_sum = sb("hat_sum", [P, P])
        diag = sb("diag", [P, P])
        junk = sb("junk", [P, P])

        ps_s = [ctx.enter_context(nc.psum_tensor(f"ps_s{i}", [P, 3 * CROWS, WINE], F32)) for i in range(2)]
        ps_t = [ctx.enter_context(nc.psum_tensor(f"ps_t{i}", [P, 512], F32)) for i in range(2)]
        ps_c = ctx.enter_context(nc.psum_tensor("ps_c", [P, 512], F32))
        ps_g = ctx.enter_context(nc.psum_tensor("ps_g", [P, 512], F32))
        ps_p = ctx.enter_context(nc.psum_tensor("ps_p", [P, 512], F32))
        ps_q = ctx.enter_context(nc.psum_tensor("ps_q", [P, 512], F32))

        def yw_at(c):
            return 0 if c == 0 else 3 if c == CHUNKS - 1 else 1 + c % 2

        def windows(b):
            return yw[:, b, :, :].rearrange("p s (r c) -> p s r c", c=WIN)

        in_par, in_w = sem("in_par"), sem("in_w")
        g_const = sem("g_const")
        g_bn = sem("g_bn")
        v_zero = sem("v_zero")
        v_w = sem("v_w")
        t_w = sem("t_w")
        v_tab = sem("v_tab")
        N_ID = 2
        N_BAND = N_ID + 1 + 3 + 4
        with nc.Block() as block:
            @block.sync
            def _(sp):
                sp.dma_start(par_s[:], par.rearrange("p (a b) -> p a b", a=3)).then_inc(in_par, 16)
                sp.dma_start(wg_s[:], wg.partition_broadcast(P)).then_inc(in_par, 16)
                for s, d in ((w1_s, w1), (w2_s, w2), (wv_s, wv), (wo_s, wo), (bo_s, bo), (bv_s, bv)):
                    sp.dma_start(s[:], d).then_inc(in_w, 16)

            @block.gpsimd
            def _(gp):
                n = [0]

                def done(instruction):
                    n[0] += 1
                    instruction.then_inc(g_const, 1)
                    gp.wait_ge(g_const, n[0])

                done(gp.memset(ident[:], 0.0))
                done(gp.affine_select(out=ident[:], in_=ident[:], compare_op=ALU.not_equal, fill=1.0,
                                      base=0, pattern=[[-1, P]], channel_multiplier=1))
                done(gp.memset(ones[:], 1.0))
                g3 = group_avg[:].rearrange("p (a b) -> p a b", b=GN)
                done(gp.memset(group_avg[:], 1.0 / GN))
                done(gp.affine_select(out=g3, in_=g3, compare_op=ALU.is_ge, fill=0.0, base=0,
                                      pattern=[[-GN, P // GN], [0, GN]], channel_multiplier=1))
                done(gp.affine_select(out=g3, in_=g3, compare_op=ALU.is_ge, fill=0.0, base=GN - 1,
                                      pattern=[[GN, P // GN], [0, GN]], channel_multiplier=-1))
                done(gp.memset(band[:], 0.0))
                for j in range(TAPS):
                    done(gp.affine_select(out=band[:, j, :], in_=band[:, j, :], compare_op=ALU.not_equal,
                                          fill=1.0, base=1 - j, pattern=[[-1, P]], channel_multiplier=1))
                assert n[0] == N_BAND
                gp.wait_ge(in_par, 32)
                k = [0]

                def bn(instruction):
                    k[0] += 1
                    instruction.then_inc(g_bn, 1)
                    gp.wait_ge(g_bn, k[0])

                bn(gp.memset(mhalf[:], -0.5))
                bn(gp.tensor_scalar(bn_w[:, 0, :], par_s[:, :, 4], EPS, None, ALU.add))
                bn(gp.tensor_tensor(bn_w[:, 1, :], bn_w[:, 0, :], mhalf[:], ALU.pow))
                bn(gp.tensor_tensor(bn_w[:, 2, :], bn_w[:, 1, :], bn_w[:, 1, :], ALU.mult))
                bn(gp.tensor_tensor(bn_w[:, 2, :], bn_w[:, 2, :], bn_w[:, 0, :], ALU.mult))
                bn(gp.tensor_scalar(bn_w[:, 2, :], bn_w[:, 2, :], -0.5, 1.5, ALU.mult, ALU.add))
                bn(gp.tensor_tensor(bn_w[:, 1, :], bn_w[:, 1, :], bn_w[:, 2, :], ALU.mult))
                bn(gp.tensor_tensor(bn_s[:], bn_w[:, 1, :], par_s[:, :, 1], ALU.mult))
                bn(gp.tensor_tensor(bn_w[:, 3, :], par_s[:, :, 0], par_s[:, :, 3], ALU.subtract))
                bn(gp.tensor_tensor(bn_w[:, 3, :], bn_w[:, 3, :], bn_s[:], ALU.mult))
                bn(gp.tensor_tensor(bn_t[:], bn_w[:, 3, :], par_s[:, :, 2], ALU.add))
                bn(gp.tensor_scalar(nbd[:], wg_s[:, 12:13], -1.0, None, ALU.mult))
                done(gp.iota(iota_i[:], pattern=[[1, P]], base=0, channel_multiplier=0))
                done(gp.tensor_copy(iota_f[:], iota_i[:]))
                done(gp.iota(base_i[:], pattern=[[1, TAPS]], base=-1, channel_multiplier=1))
                done(gp.tensor_copy(base_f[:], base_i[:]))
                done(gp.memset(mask[:], NEG))
                taps = {(i * d, j * d) for d in (1, 2, 4) for i in (-1, 0, 1) for j in (-1, 0, 1)}
                for dr, dc in sorted(taps):
                    m = mask[:, :, HALO + dc:HALO + dc + SW]
                    done(gp.affine_select(out=m, in_=m, compare_op=ALU.not_equal,
                                          fill=LN3 if dr == dc == 0 else 0.0, base=SW * (HALO + dr),
                                          pattern=[[-SW, 3 * CROWS], [-1, SW]], channel_multiplier=1))

            @block.vector
            def _(dve):
                nc.vector.memset(yw[:], 0.0).then_inc(v_zero, 1)
                dve.wait_ge(v_zero, 1)
                for b, rows in ((0, slice(HALO, CROWS)), (1, slice(0, CROWS)), (3, slice(0, HALO))):
                    for strips, cols in YW_PARTS:
                        last = nc.vector.memset(windows(b)[0:1, strips, rows, cols], 1.0)
                last.then_inc(v_zero, 1)
                nc.vector.memset(kh[:].bitcast(F32), 0.0)
                nc.vector.memset(kl[:].bitcast(F32), 0.0)
                nc.vector.memset(qq[:].bitcast(F32), 0.0)
                nc.vector.memset(v[:, :, :, HD:VCOLS], 1.0)
                nc.vector.memset(woT[:], 0.0).then_inc(v_zero, 1)
                dve.wait_ge(g_bn, 12)
                dve.wait_ge(in_w, 96)
                nc.vector.tensor_scalar(w1_s[:], w1_s[:], bn_s[:, 0:1], None, ALU.mult).then_inc(v_w, 1)
                nc.vector.tensor_scalar(w2_s[:, 0:HD], w2_s[:, 0:HD], bn_s[:, 1:2], None, ALU.mult).then_inc(v_w, 1)
                nc.vector.tensor_scalar(w2_s[:, HD:P], w2_s[:, HD:P], bn_s[:, 2:3], None, ALU.mult).then_inc(v_w, 1)
                dve.wait_ge(g_const, N_BAND)
                for k in range(TAPS):
                    nc.vector.tensor_scalar(conv[:, k, :], band[:, 0, :], wg_s[:, 3 * k:3 * k + 1], None,
                                            ALU.mult).then_inc(v_w, 1)
                for j in (1, 2):
                    dve.wait_ge(v_w, 3 + 3 * j)
                    for k in range(TAPS):
                        nc.vector.scalar_tensor_tensor(conv[:, k, :], band[:, j, :],
                                                       wg_s[:, 3 * k + j:3 * k + j + 1], conv[:, k, :],
                                                       ALU.mult, ALU.add).then_inc(v_w, 1)
                dve.wait_ge(t_w, 1)
                nc.vector.tensor_copy(w1T[:], ps_p[:, 0:P]).then_inc(v_tab, 1)
                nc.vector.tensor_copy(w2T[:], ps_p[:, P:2 * P]).then_inc(v_tab, 1)
                nc.vector.tensor_copy(wvT[:], ps_p[:, 2 * P:2 * P + HD]).then_inc(v_tab, 1)
                dve.wait_ge(v_zero, 3)
                nc.vector.tensor_copy(woT[0:HD, 0, :], ps_p[0:HD, 320:320 + P]).then_inc(v_tab, 1)
                nc.vector.tensor_copy(woT[HD:P, 1, :], ps_p[HD:P, 320:320 + P]).then_inc(v_tab, 1)
                dve.wait_ge(t_w, 2)
                for i, bank in enumerate((ps_t[0], ps_t[1], ps_c)):
                    nc.vector.tensor_copy(vbias[0:CKEYS, i, :, :].rearrange("p a b -> p (a b)"),
                                          bank[0:CKEYS, :]).then_inc(v_tab, 1)

            @block.tensor
            def _(pe):
                pe.wait_ge(g_const, N_ID)
                pe.wait_ge(v_w, 3)
                nc.tensor.transpose(ps_p[:, 0:P], w1_s[:], ident[:])
                nc.tensor.transpose(ps_p[:, P:2 * P], w2_s[:], ident[:])
                nc.tensor.transpose(ps_p[:, 2 * P:2 * P + HD], wv_s[:], ident[0:HD, 0:HD])
                nc.tensor.transpose(ps_p[:, 320:320 + P], wo_s[:], ident[:]).then_inc(t_w, 1)
                pe.wait_ge(v_zero, 2)
                for bank, b in ((ps_t[0], 0), (ps_t[1], 1), (ps_c, 3)):
                    for s in range(STRIPS):
                        last = nc.tensor.matmul(bank[0:CKEYS, s * HD:(s + 1) * HD], yw[0:1, b, s, :],
                                                bv_s[0:1, :], start=True, stop=True)
                last.then_inc(t_w, 1)

        events = []

        def event(name, per, step=1):
            events.append(Event(sem(name), per, step))
            return events[-1]

        x_in = [event("x_in0", 16, 2), event("x_in1", 16, 2)]
        stored = [event("stored0", 32), event("stored1", 32)]
        s_done = event("s_done", TILES)
        z_done = event("z_done", TILES)
        e_done = event("e_done", TILES)
        t_done = event("t_done", TILES)
        eT_done = event("eT_done", TILES)
        c_done = event("c_done", TILES)
        rd_done = event("rd_done", GROUPS)
        cx_done = event("cx_done", GROUPS)
        cT_ps = event("cT_ps", GROUPS)
        cT_done = event("cT_done", GROUPS)
        o_ps = event("o_ps", GROUPS)
        o_done = event("o_done", GROUPS)
        yw_done = event("yw_done", CHUNKS)
        y_done = event("y_done", UNITS)
        x1_done = event("x1_done", UNITS)
        h_ps = event("h_ps", UNITS)
        h_done = event("h_done", UNITS)
        q_ps = event("q_ps", UNITS)
        tq_done = event("tq_done", UNITS)
        k_ps = event("k_ps", UNITS)
        tk_done = event("tk_done", UNITS)
        qk_done = event("qk_done", 4 * UNITS)
        v_ps = event("v_ps", CHUNKS)
        v_done = event("v_done", CHUNKS)
        bs_done = event("bs_done", UNITS)
        dg, pg, cg, ag = event("dg", N_DG), event("pg", N_PG), event("cg", N_CG), event("ag", N_AG)

        def units_at(n, t):
            for m, rel in ((n, t), (n + 1, t - TILES)):
                if m.exists():
                    for u, at in enumerate(Y_SLOT):
                        if 0 <= rel - at <= 6:
                            yield m, u, rel - at

        def chain_at(n, t):
            for m, rel in ((n + 2, t), (n + 1, t + TILES)):
                if m.exists():
                    yield m, rel

        D, SQ, VE, R, T0, PL, POS, ZS, EX, GATE, RG, A_, M1, AV, D1, SQ1, VE1, R1, B_, YA, YB, M1G = (
            0, 1, 2, 3, 4, 5, 6, 9, 10, 11, 12, 13, 14, 15, 16, 17, 18, 19, 20, 21, 22, 23)
        X_A, X_B, Y_A, Y_B = 24, 26, 28, 30

        def col(c, n=1):
            return g1[:, c:c + n]

        def images(first, last, drain=0, register=None):
            with nc.Block() as block:
                @block.sync
                def _(sp):
                    def store(m, b):
                        rows = min(16, H - 16 * b)
                        sp.wait_ge(o_done.sem, o_done.count(m, 2 * b + 2))
                        sp.dma_start(out[m.index(), :, 16 * b * W:(16 * b + rows) * W],
                                     ost[:, b % 2, 0:rows, :].rearrange("p a b -> p (a b)")).then_inc(stored[b % 2].next(16), 16)

                    def slot(n, t):
                        if t == 4 and (n + -1).exists():
                            store(n + -1, 3)
                        m = n + 2
                        if t == 9 and m.exists():
                            if n.exists():
                                sp.wait_ge(yw_done.sem, yw_done.count(n, CHUNKS))
                                sp.wait_ge(x1_done.sem, x1_done.count(n, UNITS))
                                sp.wait_ge(y_done.sem, y_done.count(n, UNITS))
                            sp.dma_start(raw[:, m.parity(), :], x_d[m.index(), :, :]).then_inc(x_in[m.parity()].next(16), 16)
                        if t in (12, 20, 28) and n.exists():
                            store(n, (t - 12) // 8)

                    for n, t in slots(first, last, drain, register):
                        slot(n, t)
                    for transfers in x_in + stored:
                        sp.wait_ge(transfers.sem, transfers.here)

                @block.tensor
                def _(pe):
                    def scores(n, t):
                        b, s, rows, _ = tile(t)
                        if t % STRIPS == 0:
                            pe.wait_ge(qk_done.sem, qk_done.count(n, 4 * BAND_UNITS[b]))
                        pe.wait_ge(z_done.sem, z_done.count(n, t - 1))
                        o = ps_s[t % 2][0:MAXQ, 0:rows + CROWS, :]
                        k = slice(16 * b, 16 * b + rows + CROWS)
                        cols = slice(SW * s, SW * s + WINE)
                        nc.tensor.matmul(o, qq[:, t, :], kh[:, k, cols], start=True, stop=False)
                        nc.tensor.matmul(o, qq[0:HD, t, :], kl[:, k, cols], start=False,
                                         stop=True).then_inc(s_done.next(), 1)

                    def transposed(n, t):
                        _, _, rows, nq = tile(t)
                        pe.wait_ge(e_done.sem, e_done.count(n, t + 1))
                        pe.wait_ge(eT_done.sem, eT_done.count(n, t - 1))
                        for i in range(len(window_chunks(t))):
                            last = nc.tensor.transpose(ps_t[t % 2][0:CKEYS, i * nq:(i + 1) * nq],
                                                       e[0:nq, t % 2, i * CKEYS:(i + 1) * CKEYS], ident[0:nq, 0:nq])
                        last.then_inc(t_done.next(), 1)

                    def context(n, t):
                        b, s, _, nq = tile(t)
                        if t % STRIPS == 0:
                            pe.wait_ge(v_done.sem, v_done.count(n, BAND_CHUNKS[b]))
                        pe.wait_ge(eT_done.sem, eT_done.count(n, t + 1))
                        g, j = divmod(t, TPG)
                        pe.wait_ge(cx_done.sem, cx_done.count(n, g))
                        chunks = window_chunks(t)
                        for i, c in enumerate(chunks):
                            last = nc.tensor.matmul(ps_c[0:nq, j * VCOLS:(j + 1) * VCOLS],
                                                    eT[:, t % 2, i * nq:(i + 1) * nq], v[:, c, s, :],
                                                    start=(i == 0), stop=(i == len(chunks) - 1))
                        last.then_inc(c_done.next(), 1)

                    def context_transposed(n, g):
                        nq = tile(g * TPG)[3]
                        pe.wait_ge(cx_done.sem, cx_done.count(n, g + 1))
                        pe.wait_ge(o_done.sem, o_done.count(n, g))
                        for h in range(2):
                            last = nc.tensor.transpose(ps_g[:, h * nq:(h + 1) * nq],
                                                       cx[0:nq, 2 * h:2 * h + 2, :].rearrange("p a b -> p (a b)"),
                                                       ident[0:nq, 0:nq])
                        last.then_inc(cT_ps.next(), 1)

                    def output(n, g):
                        nq = tile(g * TPG)[3]
                        pe.wait_ge(cT_done.sem, cT_done.count(n, g + 1))
                        o = ps_g[:, 0:4 * nq].rearrange("p (h a q) -> p h a q", h=2, a=2)
                        for a in range(2):
                            last = nc.tensor.matmul(o[:, :, a, :], woT[:, a, :], cT[:, :, 0:nq], start=True, stop=True)
                        last.then_inc(o_ps.next(), 1)

                    def hidden(m, u):
                        pe.wait_ge(y_done.sem, y_done.count(m, u + 1))
                        pe.wait_ge(v_done.sem, v_done.count(m, u))
                        nc.tensor.matmul(ps_p[:, 0:UPIX], w1T[:], y[:, (m.parity() + u) % 2, :], start=True,
                                         stop=True).then_inc(h_ps.next(), 1)

                    def query(m, u):
                        pe.wait_ge(h_done.sem, h_done.count(m, u + 1))
                        nc.tensor.matmul(ps_p[:, 0:UPIX], w2T[0:HD, :], hid[0:HD, :, :], start=True,
                                         stop=True).then_inc(q_ps.next(), 1)

                    def key(m, u):
                        pe.wait_ge(tq_done.sem, tq_done.count(m, u + 1))
                        nc.tensor.matmul(ps_p[:, 0:UPIX], w2T[HD:P, :], hid[HD:P, :, :], start=True,
                                         stop=True).then_inc(k_ps.next(), 1)

                    def values(m, c):
                        pe.wait_ge(yw_done.sem, yw_done.count(m, c + 1))
                        if c < UNITS:
                            pe.wait_ge(tk_done.sem, tk_done.count(m, c + 1))
                        else:
                            pe.wait_ge(v_done.sem, v_done.count(m, c))
                        for s in range(STRIPS):
                            last = nc.tensor.matmul(ps_p[0:CKEYS, s * HD:(s + 1) * HD], yw[:, yw_at(c), s, :], wvT[:],
                                                    start=True, stop=True)
                        last.then_inc(v_ps.next(), 1)

                    def chain(m, at):
                        def avg(k, src, ready, to):
                            pe.wait_ge(dg.sem, dg.count(m, ready))
                            nc.tensor.matmul(ps_q[:, to:to + 1], group_avg[:], src, start=True,
                                             stop=True).then_inc(cg.next(), 1)
                        if at == CH["c1"]:
                            avg(1, st[:, 0:1], 1, 0)
                        if at == CH["c2"]:
                            avg(2, col(SQ), 3, 1)
                        if at == CH["c3"]:
                            pe.wait_ge(pg.sem, pg.count(m, 7))
                            for k in range(TAPS):
                                nc.tensor.matmul(ps_q[:, 4 + k:5 + k], conv[:, k, :], col(PL), start=True, stop=True)
                            nc.tensor.matmul(ps_q[:, P:2 * P], ones[:], diag[:], start=True, stop=True).then_inc(cg.next(), 1)
                        if at == CH["c4"]:
                            pe.wait_ge(pg.sem, pg.count(m, 20))
                            nc.tensor.matmul(ps_q[:, 2:3], group_avg[:], col(M1), start=True, stop=True).then_inc(cg.next(), 1)
                        if at == CH["c5"]:
                            avg(5, col(SQ1), 11, 3)

                    def slot(n, t):
                        if n.exists():
                            scores(n, t)
                        for lag, work in ((1, transposed), (2, context)):
                            m, k = lagged(n, t, lag)
                            if m.exists():
                                work(m, k)
                        m, k = lagged(n, t, 6)
                        if k % TPG == 0 and m.exists():
                            context_transposed(m, k // TPG)
                        m, k = lagged(n, t, 7)
                        if k % TPG == 0 and m.exists():
                            output(m, k // TPG)
                        for m, u, since in units_at(n, t):
                            if since == 1:
                                hidden(m, u)
                            if since == 2:
                                query(m, u)
                            if since == 3:
                                key(m, u)
                            if since == 4:
                                values(m, u)
                            if since == 5 and u == UNITS - 1:
                                values(m, u + 1)
                        for m, at in chain_at(n, t):
                            chain(m, at)

                    for n, t in slots(first, last, drain, register):
                        slot(n, t)

                @block.scalar
                def _(act):
                    def exponentials(n, t):
                        _, _, rows, nq = tile(t)
                        keys = (rows + CROWS) * WIN
                        act.wait_ge(z_done.sem, z_done.count(n, t + 1))
                        act.wait_ge(t_done.sem, t_done.count(n, t - 1))
                        nc.scalar.activation(e[0:nq, t % 2, 0:keys], z[0:nq, t % 2, 0:keys], ACT.Exp,
                                             bias=zmin[0:nq, t % 2:t % 2 + 1], scale=-1.0).then_inc(e_done.next(), 1)

                    def copy(n, t):
                        _, _, _, nq = tile(t)
                        cols = nq * len(window_chunks(t))
                        act.wait_ge(t_done.sem, t_done.count(n, t + 1))
                        act.wait_ge(c_done.sem, c_done.count(n, t - 1))
                        nc.scalar.activation(eT[:, t % 2, 0:cols], ps_t[t % 2][0:CKEYS, 0:cols],
                                             ACT.Copy).then_inc(eT_done.next(), 1)

                    def relu(to, column):
                        return nc.scalar.activation(to[:].rearrange("p a b -> p (a b)"), ps_p[:, 0:UPIX], ACT.Relu,
                                                    bias=bn_t[:, column:column + 1])

                    def slot(n, t):
                        if n.exists():
                            exponentials(n, t)
                        m, k = lagged(n, t, 1)
                        if m.exists():
                            copy(m, k)
                        for m, u, since in units_at(n, t):
                            if since == 1:
                                act.wait_ge(h_ps.sem, h_ps.count(m, u + 1))
                                act.wait_ge(k_ps.sem, k_ps.count(m, u))
                                relu(hid, 0).then_inc(h_done.next(), 1)
                            if since == 2:
                                act.wait_ge(q_ps.sem, q_ps.count(m, u + 1))
                                act.wait_ge(qk_done.sem, qk_done.count(m, 4 * u))
                                relu(tq, 1).then_inc(tq_done.next(), 1)
                            if since == 3:
                                act.wait_ge(k_ps.sem, k_ps.count(m, u + 1))
                                act.wait_ge(qk_done.sem, qk_done.count(m, 4 * u))
                                relu(tk, 2).then_inc(tk_done.next(), 1)
                        for m, at in chain_at(n, t):
                            if at == CH["d4"]:
                                act.wait_ge(dg.sem, dg.count(m, 6))
                                act.wait_ge(pg.sem, pg.count((m + -1), 13))
                                for k in range(TAPS):
                                    nc.scalar.activation(hats[:, k, 0, :], iota_f[:], ACT.Abs, bias=col(POS + k),
                                                         scale=-1.0).then_inc(ag.next(), 1)
                            if at == CH["d6"]:
                                act.wait_ge(dg.sem, dg.count(m, 7))
                                nc.scalar.activation(col(EX), col(ZS), ACT.Exp, bias=nbd[:, 0:1],
                                                     scale=-1.0).then_inc(ag.next(), 1)

                    for n, t in slots(first, last, drain, register):
                        slot(n, t)

                @block.gpsimd
                def _(gp):
                    def chain(m, at):
                        def steps(first, *instructions):
                            for i, make in enumerate(instructions):
                                gp.wait_ge(pg.sem, pg.count(m, first + i))
                                make().then_inc(pg.next(), 1)

                        def rsqrt(to, ve, t):
                            return (lambda: gp.tensor_tensor(to, ve, mhalf[:, 0:1], ALU.pow),
                                    lambda: gp.tensor_tensor(t, to, to, ALU.mult),
                                    lambda: gp.tensor_tensor(t, t, ve, ALU.mult),
                                    lambda: gp.tensor_scalar(t, t, -0.5, 1.5, ALU.mult, ALU.add),
                                    lambda: gp.tensor_tensor(to, to, t, ALU.mult))
                        if at == CH["d3"]:
                            gp.wait_ge(dg.sem, dg.count(m, 4))
                            steps(0, *rsqrt(col(R), col(VE), col(T0)),
                                  lambda: gp.tensor_tensor(col(PL), col(D), col(R), ALU.mult),
                                  lambda: gp.tensor_scalar(diag[:], ident[:], col(PL), None, ALU.mult))
                        if at == CH["d4"]:
                            gp.wait_ge(ag.sem, ag.count(m, 3))

                            def tap(k):
                                far, hat = hats[:, k, 0, :], hats[:, k, 1, :]
                                return (lambda: gp.tensor_scalar(hat, far, -1.0, 1.0, ALU.mult, ALU.add),
                                        lambda: gp.tensor_scalar(hat, hat, 0.0, wg_s[:, 9 + k:10 + k], ALU.max, ALU.mult))
                            steps(7, *tap(0), *tap(1), *tap(2),
                                  lambda: gp.tensor_tensor(hat_sum[:], hats[:, 0, 1, :], hats[:, 1, 1, :], ALU.add),
                                  lambda: gp.tensor_tensor(hat_sum[:], hat_sum[:], hats[:, 2, 1, :], ALU.add))
                        if at == CH["d7"]:
                            gp.wait_ge(dg.sem, dg.count(m, 9))
                            steps(15,
                                  lambda: gp.tensor_tensor(col(RG), col(R), col(GATE), ALU.mult),
                                  lambda: gp.tensor_scalar(col(A_), col(RG), 1.0, None, ALU.add),
                                  lambda: gp.tensor_tensor(col(T0), col(RG), col(D), ALU.mult),
                                  lambda: gp.tensor_tensor(col(AV), col(A_), col(A_), ALU.mult),
                                  lambda: gp.tensor_tensor(col(M1), col(T0), st[:, 0:1], ALU.add),
                                  lambda: gp.tensor_tensor(col(AV), col(AV), st[:, 1:2], ALU.mult),
                                  lambda: gp.tensor_tensor(col(M1G), st[:, 0:1], col(D), ALU.subtract),
                                  lambda: gp.tensor_tensor(col(M1G), col(M1G), col(RG), ALU.mult))
                        if at == CH["d11"]:
                            gp.wait_ge(dg.sem, dg.count(m, 12))
                            gp.wait_ge(y_done.sem, y_done.count(m + -1, 0))
                            gp.wait_ge(x1_done.sem, x1_done.count(m + -1, 0))
                            steps(23, *rsqrt(col(R1), col(VE1), col(T0)),
                                  lambda: gp.tensor_tensor(col(YA), col(A_), col(R1), ALU.mult),
                                  lambda: gp.tensor_tensor(col(T0), col(D1), col(M1), ALU.subtract),
                                  lambda: gp.tensor_tensor(col(T0), col(T0), col(M1G), ALU.subtract),
                                  lambda: gp.tensor_tensor(col(YB), col(T0), col(R1), ALU.mult),
                                  lambda: gp.tensor_tensor(col(B_), bo_s[:], col(M1G), ALU.subtract),
                                  lambda: gp.tensor_scalar(col(X_A + m.parity()), col(A_), 1.0, None, ALU.mult),
                                  lambda: gp.tensor_scalar(col(X_B + m.parity()), col(B_), 1.0, None, ALU.mult),
                                  lambda: gp.tensor_scalar(col(Y_A + m.parity()), col(YA), 1.0, None, ALU.mult),
                                  lambda: gp.tensor_scalar(col(Y_B + m.parity()), col(YB), 1.0, None, ALU.mult))

                    def chunk_windows(m, c):
                        gp.wait_ge(v_ps.sem, v_ps.count(m, c))
                        if c == 0:
                            gp.wait_ge(pg.sem, pg.count(m, N_PG))
                        r0, r1 = max(0, CROWS * c - HALO), min(H, CROWS * (c + 1) - HALO)
                        w0 = r0 - (CROWS * c - HALO)
                        for strips, cols in YW_PARTS:
                            ns, nw = strips.stop - strips.start, cols.stop - cols.start
                            x0 = SW * strips.start + cols.start - HALO
                            rows = raw[:, m.parity(), W * r0:W * r1]
                            src = bass.AP(rows.tensor, rows.offset + x0,
                                          [list(rows.ap[0]), [SW, ns], [W, r1 - r0], [1, nw]])
                            last = gp.tensor_scalar(windows(yw_at(c))[:, strips, w0:w0 + r1 - r0, cols], src,
                                                    col(Y_A + m.parity()), col(Y_B + m.parity()), ALU.mult, ALU.add)
                        last.then_inc(yw_done.next(), 1)

                    def slot(n, t):
                        for m, u, since in units_at(n, t):
                            prow = slice(HALO + UROWS * u, HALO + UROWS * (u + 1))
                            pcol = slice(HALO, HALO + W)
                            if since == 1:
                                chunk_windows(m, u)
                            if since == 2:
                                gp.wait_ge(tq_done.sem, tq_done.count(m, u + 1))
                                b, half = divmod(u, 2)
                                tiles = qq[:, STRIPS * b:STRIPS * (b + 1), UROWS * SW * half:UROWS * SW * (half + 1)
                                           ].rearrange("p s (r c) -> p r s c", c=SW)
                                src = tq[:].rearrange("p r (s c) -> p r s c", c=SW)
                                gp.tensor_scalar(tiles, src, 1.0, None, ALU.mult).then_inc(qk_done.next(), 1)
                                gp.wait_ge(qk_done.sem, qk_done.count(m, 4 * u + 1))
                                gp.tensor_tensor(tiles[HD:P], src[HD:P], tiles[HD:P].bitcast(F32),
                                                 ALU.subtract).then_inc(qk_done.next(), 1)
                                gp.wait_ge(qk_done.sem, qk_done.count(m, 4 * u + 2))
                            if since == 3:
                                gp.wait_ge(tk_done.sem, tk_done.count(m, u + 1))
                                gp.tensor_scalar(kh[:, prow, pcol], tk[:], 1.0, None, ALU.mult).then_inc(qk_done.next(), 1)
                                gp.wait_ge(qk_done.sem, qk_done.count(m, 4 * u + 3))
                                gp.tensor_tensor(kl[:, prow, pcol], tk[0:HD], kh[0:HD, prow, pcol].bitcast(F32),
                                                 ALU.subtract).then_inc(qk_done.next(), 1)
                                gp.wait_ge(qk_done.sem, qk_done.count(m, 4 * u + 4))
                            if since == 4 and u == UNITS - 1:
                                chunk_windows(m, u + 1)
                        for m, at in chain_at(n, t):
                            chain(m, at)

                    for n, t in slots(first, last, drain, register):
                        slot(n, t)

                @block.vector
                def _(dve):
                    def masked(n, t):
                        _, _, rows, nq = tile(t)
                        wr = rows + CROWS
                        dve.wait_ge(s_done.sem, s_done.count(n, t + 1))
                        dve.wait_ge(e_done.sem, e_done.count(n, t - 1))
                        nc.vector.tensor_tensor_reduce(
                            z[0:nq, t % 2, 0:wr * WIN].rearrange("p (a b) -> p a b", b=WIN),
                            ps_s[t % 2][0:nq, 0:wr, 0:WIN], mask[0:nq, 0:wr, :], scale=-1.0, scalar=3e38,
                            op0=ALU.add, op1=ALU.min, accum_out=zmin[0:nq, t % 2:t % 2 + 1]).then_inc(z_done.next(), 1)

                    def normalised(n, g):
                        nq = tile(g * TPG)[3]
                        dve.wait_ge(c_done.sem, c_done.count(n, TPG * (g + 1)))
                        dve.wait_ge(cT_ps.sem, cT_ps.count(n, g))
                        c = ps_c[0:nq, 0:TPG * VCOLS].rearrange("p (a b) -> p a b", b=VCOLS)
                        nc.vector.reciprocal(rden[0:nq, :], c[:, :, HD]).then_inc(rd_done.next(), 1)
                        dve.wait_ge(rd_done.sem, rd_done.count(n, g + 1))
                        nc.vector.tensor_tensor(cx[0:nq, :, :], c[:, :, 0:HD],
                                                rden[0:nq, :].unsqueeze(2).to_broadcast([nq, TPG, HD]),
                                                ALU.mult).then_inc(cx_done.next(), 1)

                    def context_copy(n, g):
                        nq = tile(g * TPG)[3]
                        dve.wait_ge(cT_ps.sem, cT_ps.count(n, g + 1))
                        dve.wait_ge(o_ps.sem, o_ps.count(n, g))
                        nc.vector.tensor_copy(cT[:, :, 0:nq], ps_g[:, 0:2 * nq].rearrange("p (a b) -> p a b", a=2)
                                              ).then_inc(cT_done.next(), 1)

                    def final(n, g):
                        b, s, rows, nq = tile(g * TPG)
                        dve.wait_ge(o_ps.sem, o_ps.count(n, g + 1))
                        dve.wait_ge(stored[b % 2].sem, stored[b % 2].count(n, 16 * (b // 2)))

                        def part(t):
                            return t[:, :, SW * s:SW * (s + TPG)].rearrange("p h (a w) -> p a h w", w=SW)
                        nc.vector.tensor_tensor(part(ost[:, b % 2, 0:rows, :]),
                                                ps_g[:, 0:TPG * nq].rearrange("p (a h w) -> p a h w", a=TPG, w=SW),
                                                part(x1[:, 16 * b:16 * b + rows, :]), ALU.add).then_inc(o_done.next(), 1)

                    def values_copy(m, c):
                        dve.wait_ge(v_ps.sem, v_ps.count(m, c + 1))
                        kind = 0 if c == 0 else 2 if c == CHUNKS - 1 else 1
                        nc.vector.tensor_tensor(v[:, c, :, 0:HD],
                                                ps_p[0:CKEYS, :].rearrange("p (a b) -> p a b", b=HD),
                                                vbias[0:CKEYS, kind, :, :], ALU.add).then_inc(v_done.next(), 1)

                    def normed(m, u):
                        px = slice(UPIX * u, UPIX * (u + 1))
                        src = raw[:, m.parity(), px]
                        if u == 0:
                            dve.wait_ge(pg.sem, pg.count(m, N_PG))
                        dve.wait_ge(h_ps.sem, h_ps.count(m, u - 1))
                        nc.vector.tensor_scalar(y[:, (m.parity() + u) % 2, :], src,
                                                col(Y_A + m.parity()), col(Y_B + m.parity()), ALU.mult, ALU.add).then_inc(y_done.next(), 1)
                        dve.wait_ge(o_done.sem, o_done.count((m + -1), [2, 2, 4, 4, 6, 6, 8][u]))
                        nc.vector.tensor_scalar(x1[:, UROWS * u:UROWS * (u + 1), :].rearrange("p a b -> p (a b)"), src,
                                                col(X_A + m.parity()), col(X_B + m.parity()), ALU.mult, ALU.add).then_inc(x1_done.next(), 1)

                    def chain(m, at):
                        def step(k, instruction):
                            instruction.then_inc(dg.next(), 1)
                            dve.wait_ge(dg.sem, dg.count(m, k))

                        i = at - CH["stats"]
                        if 0 <= i < UNITS:
                            if i == 0:
                                dve.wait_ge(x_in[m.parity()].sem, x_in[m.parity()].count(m, 16))
                                dve.wait_ge(dg.sem, dg.count(m, 0))
                            nc.vector.bn_stats(stats[:, i, :], raw[:, m.parity(), UPIX * i:UPIX * (i + 1)]
                                               ).then_inc(bs_done.next(), 1)
                        if at == CH["aggr"]:
                            dve.wait_ge(bs_done.sem, bs_done.count(m, UNITS))
                            step(1, nc.vector.bn_aggr(st[:], stats[:].rearrange("p a b -> p (a b)")))
                        if at == CH["d1"]:
                            dve.wait_ge(cg.sem, cg.count(m, 1))
                            step(2, nc.vector.tensor_tensor(col(D), st[:, 0:1], ps_q[:, 0:1], ALU.subtract))
                            step(3, nc.vector.scalar_tensor_tensor(col(SQ), col(D), col(D), st[:, 1:2],
                                                                   ALU.mult, ALU.add))
                        if at == CH["d3"]:
                            dve.wait_ge(cg.sem, cg.count(m, 2))
                            step(4, nc.vector.tensor_scalar(col(VE), ps_q[:, 1:2], EPS, None, ALU.add))
                        if at == CH["d4"]:
                            dve.wait_ge(cg.sem, cg.count(m, 3))
                            step(5, nc.vector.tensor_tensor(col(POS, 3), ps_q[:, 4:7], base_f[:], ALU.add))
                            step(6, nc.vector.tensor_scalar(col(POS, 3), col(POS, 3), 0.0, P - 1.0, ALU.max, ALU.min))
                        if at == CH["d6"]:
                            dve.wait_ge(pg.sem, pg.count(m, 15))
                            step(7, nc.vector.scalar_tensor_tensor(junk[:], ps_q[:, P:2 * P], 1.0, hat_sum[:],
                                                                   ALU.mult, ALU.mult, accum_out=col(ZS)))
                        if at == CH["d7"]:
                            dve.wait_ge(ag.sem, ag.count(m, 4))
                            step(8, nc.vector.tensor_scalar(col(EX), col(EX), 1.0, None, ALU.add))
                            step(9, nc.vector.reciprocal(col(GATE), col(EX)))
                        if at == CH["d9"]:
                            dve.wait_ge(cg.sem, cg.count(m, 4))
                            step(10, nc.vector.tensor_tensor(col(D1), col(M1), ps_q[:, 2:3], ALU.subtract))
                            dve.wait_ge(pg.sem, pg.count(m, 23))
                            step(11, nc.vector.scalar_tensor_tensor(col(SQ1), col(D1), col(D1), col(AV),
                                                                    ALU.mult, ALU.add))
                        if at == CH["d11"]:
                            dve.wait_ge(cg.sem, cg.count(m, 5))
                            step(12, nc.vector.tensor_scalar(col(VE1), ps_q[:, 3:4], EPS, None, ALU.add))

                    def slot(n, t):
                        if n.exists():
                            masked(n, t)
                        m, k = lagged(n, t, 7)
                        if k % TPG == 0 and m.exists():
                            context_copy(m, k // TPG)
                        m, k = lagged(n, t, 8)
                        if k % TPG == 0 and m.exists():
                            final(m, k // TPG)
                        for m, u, since in units_at(n, t):
                            if since == 0:
                                normed(m, u)
                            if since == 5:
                                values_copy(m, u)
                            if since == 6 and u == UNITS - 1:
                                values_copy(m, u + 1)
                        for m, at in chain_at(n, t):
                            chain(m, at)
                        m, k = lagged(n, t, 5)
                        if k % TPG == 0 and m.exists():
                            normalised(m, k // TPG)

                    for n, t in slots(first, last, drain, register):
                        slot(n, t)

        def restart(rounds=1):
            for e in events:
                e.end_part(rounds)
            with nc.Block() as block:
                @block.gpsimd
                def _(gp):
                    for e in events:
                        gp.sem_clear(e.sem)

        images(-2, 1)
        restart()
        with nc.Fori(0, ROUNDS) as i:
            images(2, 1 + PAIR, register=i)
            restart(ROUNDS)
        images(NIMG - 2, NIMG - 1, drain=5)


def kernel(**inputs):
    import numpy as _np
    import concourse.bacc as _bacc
    from concourse import mybir as _mybir
    from concourse.bass_utils import run_bass_kernel_spmd as _run

    a = {k.replace("L1_conv_", "").replace("L0_conv_", ""): _np.asarray(v) for k, v in inputs.items()}
    x = a["x"]

    def stacked(top, bottom, layer):
        return _np.stack([_np.concatenate([a[f"{top}{layer}_{p}"], a[f"{bottom}{layer}_{p}"]])
                          for p in ("b", "g", "be", "m", "v")], axis=1)
    w2 = _np.concatenate([a["q2_w"], a["k2_w"]], axis=1)
    arrays = {
        "x": x.reshape(NIMG, P, H * W),
        "par": _np.concatenate([stacked("q", "k", 1), stacked("q", "q", 2), stacked("k", "k", 2)], axis=1),
        "w1": _np.concatenate([a["q1_w"], a["k1_w"]], axis=0),
        "w2": _np.concatenate([w2, w2], axis=0),
        "wv": a["v_w"],
        "wo": _np.concatenate([a["w_w"], a["w_w"]], axis=1),
        "bo": a["w_b"].reshape(P, 1),
        "bv": a["v_b"].reshape(1, HD),
        "wg": _np.concatenate([a["w_offset"].reshape(-1), a["w_deform"].reshape(-1), a["b_deform"].reshape(-1)]),
    }
    nc = _bacc.Bacc("TRN2", target_bir_lowering=False, num_devices=1)
    arrays = {f"in_{k}_dram": _np.ascontiguousarray(t) for k, t in arrays.items()}
    args = [nc.dram_tensor(k, t.shape, _mybir.dt.from_np(t.dtype), kind="ExternalInput").ap()
            for k, t in arrays.items()]
    args.append(nc.dram_tensor("out_0_dram", (NIMG, P, H * W), _mybir.dt.float32, kind="ExternalOutput").ap())
    build(nc, *args)
    r = _run(nc, [arrays], core_ids=[0])
    return r.results[0]["out_0_dram"].reshape(x.shape)
```

```python
from contextlib import ExitStack

import concourse.bass as bass
from concourse import mybir

F32 = mybir.dt.float32
F32R = mybir.dt.float32r
I32 = mybir.dt.int32
ALU = mybir.AluOpType
ACT = mybir.ActivationFunctionType

P = 128
NIMG = 32
ROUND = 4
ROUNDS = (NIMG - 4) // ROUND
H = W = 56
HALO = 4
HD = 64
UROWS = 8
UNITS = H // UROWS
UPIX = UROWS * W
PROWS = H + 2 * HALO
PCOLS = W + 2 * HALO
SW = 7
STRIPS = W // SW
WIN = SW + 2 * HALO
CROWS = 8
CHUNKS = PROWS // CROWS
CPIX = CROWS * PCOLS
CKEYS = CROWS * WIN
VCOLS = HD + 1
TILES = 4 * STRIPS
TPG = 4
GROUPS = TILES // TPG
MAXQ = 16 * SW
GN = 4
EPS = 1e-5
NEG = -1e30
LN3 = 1.0986122886681098
TAPS = 3


def tile(k):
    band, strip = divmod(k, STRIPS)
    rows = min(16, H - 16 * band)
    return band, strip, rows, rows * SW


def window_chunks(k):
    band, _, rows, _ = tile(k)
    return range(2 * band, 2 * band + (rows + 2 * HALO) // CROWS)


Y_SLOT = [-20, -16, -12, -8, -4, 0, 5]
V_SLOT = [at + 4 for at in Y_SLOT] + [10]
CHAIN_READS = ((2, "d1"), (4, "d3"), (7, "d4"), (11, "d9"), (13, "d11"))
BAND_UNITS = [3, 5, 7, 7]
BAND_CHUNKS = [3, 5, 7, 8]
CH = dict(stats=12, aggr=19, c1=22, d1=23, c2=26, d3=27, p3=28, c3=30, d4=31, a4=32, p4=33, d6=35,
          a6=36, d7=37, p7=37, c4=38, d9=39, c5=40, d11=41, p11=41)
TRANSPOSE, CONTEXT = 2, 3
NORM, CX_TRANSPOSE, CT_COPY, OUTPUT, FINAL = [TPG - 1 + CONTEXT + i for i in range(5)]
RING = 4
STORE = TPG + FINAL
DRAIN = STORE + 3 * STRIPS - TILES + 1
N_DG, N_PG, N_CG, N_AG = 13, 37, 5, 4


class Image:

    def __init__(self, offset, register=None):
        self.offset, self.register = offset, register

    def __add__(self, n):
        return Image(self.offset + n, self.register)

    def exists(self):
        return self.register is not None or 0 <= self.offset < NIMG

    def parity(self):
        return self.offset % 2

    def index(self):
        return self.offset if self.register is None else self.register * ROUND + self.offset


class Event:

    def __init__(self, sem, per, step=1):
        self.sem, self.per, self.step = sem, per, step
        self.before, self.here = 0, 0

    def next(self, n=1):
        self.here += n
        return self.sem

    def count(self, m, k):
        return max(0, m.offset // self.step * self.per + k - self.before)

    def end_part(self, rounds):
        self.before += self.here * rounds
        self.here = 0


def lagged(n, t, lag):
    return (n, t - lag) if t >= lag else (n + -1, t - lag + TILES)


def slots(first, last, drain=0, register=None):
    for o in range(first, last + 1):
        for t in range(TILES):
            yield Image(o, register), t
    for t in range(drain):
        yield Image(last + 1, register), t


def build(nc, x, par, w1, w2, wv, wo, bo, bv, wg, out):
    x_d = x.rearrange("n c p -> n c p")
    with ExitStack() as ctx:
        def sb(name, shape, dt=F32):
            return ctx.enter_context(nc.sbuf_tensor(name, shape, dt))

        def sem(name):
            return ctx.enter_context(nc.semaphore(name))

        ident = sb("ident", [P, P])
        ones = sb("ones", [P, P])
        group_avg = sb("group_avg", [P, P])
        band = sb("band", [P, TAPS, P])
        conv = sb("conv", [P, TAPS, P])
        iota_i = sb("iota_i", [P, P], I32)
        iota_f = sb("iota_f", [P, P])
        base_i = sb("base_i", [P, TAPS], I32)
        base_f = sb("base_f", [P, TAPS])
        mhalf = sb("mhalf", [P, TAPS])
        mask = sb("mask", [P, 3, WIN, CROWS])
        vbias = sb("vbias", [P, 3, STRIPS, HD])
        par_s = sb("par_s", [P, 3, 5])
        bn_s = sb("bn_s", [P, 3])
        bn_t = sb("bn_t", [P, 3])
        bn_w = sb("bn_w", [P, 4, 3])
        w1_s = sb("w1_s", [P, P])
        w2_s = sb("w2_s", [P, P])
        wv_s = sb("wv_s", [HD, P])
        wo_s = sb("wo_s", [P, P])
        bo_s = sb("bo_s", [P, 1])
        bv_s = sb("bv_s", [1, HD])
        wg_s = sb("wg_s", [P, 13])
        nbd = sb("nbd", [P, 1])
        w1T = sb("w1T", [P, P])
        w2T = sb("w2T", [P, P])
        wvT = sb("wvT", [P, HD])
        woT = sb("woT", [P, 2, P])
        raw = sb("raw", [P, 2, H * W])
        x1 = sb("x1", [P, H, W])
        yp = sb("yp", [P, CHUNKS * CPIX])
        hid = sb("hid", [P, UROWS, W])
        tq = sb("tq", [P, UPIX])
        tk = sb("tk", [P, UPIX])
        qq = sb("qq", [P, TILES, MAXQ], F32R)
        kh = sb("kh", [P, CHUNKS * CPIX], F32R)
        kl = sb("kl", [HD, CHUNKS * CPIX], F32R)
        v = sb("v", [CKEYS, CHUNKS, STRIPS, VCOLS])
        z = sb("z", [MAXQ, RING, 3 * CKEYS])
        zmin = sb("zmin", [MAXQ, RING])
        e = sb("e", [MAXQ, RING, 3 * CKEYS])
        eT = sb("eT", [CKEYS, RING, 3 * MAXQ])
        rden = sb("rden", [MAXQ, TPG])
        cx = sb("cx", [MAXQ, TPG, HD])
        cT = sb("cT", [P, 2, MAXQ])
        ost = sb("ost", [P, 2, 16, W])
        stats = sb("stats", [P, UNITS, 6])
        st = sb("st", [P, 2])
        g1 = sb("g1", [P, 48])
        hats = sb("hats", [P, TAPS, 2, P])
        hat_sum = sb("hat_sum", [P, P])
        diag = sb("diag", [P, P])
        pooled_row = sb("pooled_row", [P, P])
        junk = sb("junk", [P, P])

        ps_s = [ctx.enter_context(nc.psum_tensor(f"ps_s{i}", [P, 3, CKEYS], F32)) for i in range(2)]
        ps_t = [ctx.enter_context(nc.psum_tensor(f"ps_t{i}", [P, 512], F32)) for i in range(2)]
        ps_c = ctx.enter_context(nc.psum_tensor("ps_c", [P, 512], F32))
        ps_g = ctx.enter_context(nc.psum_tensor("ps_g", [P, 512], F32))
        ps_p = ctx.enter_context(nc.psum_tensor("ps_p", [P, 512], F32))
        ps_v = ctx.enter_context(nc.psum_tensor("ps_v", [P, 512], F32))

        def inside(buf, u, parts=slice(0, P)):
            a = buf[parts, CPIX * u:CPIX * u + 1]
            return bass.AP(a.tensor, a.offset + CROWS * HALO + HALO,
                           [list(a.ap[0]), [CPIX - HALO, 2], [1, HALO], [CROWS, W]])

        def halves(a):
            return a.rearrange("p (h r c) -> p h r c", h=2, c=W)

        def window(buf, c, strip, parts=slice(0, P)):
            return buf[parts, CPIX * c + CROWS * SW * strip:CPIX * c + CROWS * SW * strip + CKEYS]

        in_par, in_w = sem("in_par"), sem("in_w")
        g_const = sem("g_const")
        g_bn = sem("g_bn")
        v_zero = sem("v_zero")
        v_w = sem("v_w")
        t_w = sem("t_w")
        v_tab = sem("v_tab")
        N_ID = 2
        N_BAND = N_ID + 1 + 3 + 4
        with nc.Block() as block:
            @block.sync
            def _(sp):
                sp.dma_start(par_s[:], par.rearrange("p (a b) -> p a b", a=3)).then_inc(in_par, 16)
                sp.dma_start(wg_s[:], wg.partition_broadcast(P)).then_inc(in_par, 16)
                for s, d in ((w1_s, w1), (w2_s, w2), (wv_s, wv), (wo_s, wo), (bo_s, bo), (bv_s, bv)):
                    sp.dma_start(s[:], d).then_inc(in_w, 16)

            @block.gpsimd
            def _(gp):
                n = [0]

                def done(instruction):
                    n[0] += 1
                    instruction.then_inc(g_const, 1)
                    gp.wait_ge(g_const, n[0])

                done(gp.memset(ident[:], 0.0))
                done(gp.affine_select(out=ident[:], in_=ident[:], compare_op=ALU.not_equal, fill=1.0,
                                      base=0, pattern=[[-1, P]], channel_multiplier=1))
                done(gp.memset(ones[:], 1.0))
                g3 = group_avg[:].rearrange("p (a b) -> p a b", b=GN)
                done(gp.memset(group_avg[:], 1.0 / GN))
                done(gp.affine_select(out=g3, in_=g3, compare_op=ALU.is_ge, fill=0.0, base=0,
                                      pattern=[[-GN, P // GN], [0, GN]], channel_multiplier=1))
                done(gp.affine_select(out=g3, in_=g3, compare_op=ALU.is_ge, fill=0.0, base=GN - 1,
                                      pattern=[[GN, P // GN], [0, GN]], channel_multiplier=-1))
                done(gp.memset(band[:], 0.0))
                for j in range(TAPS):
                    done(gp.affine_select(out=band[:, j, :], in_=band[:, j, :], compare_op=ALU.not_equal,
                                          fill=1.0, base=1 - j, pattern=[[-1, P]], channel_multiplier=1))
                assert n[0] == N_BAND
                gp.wait_ge(in_par, 32)
                k = [0]

                def bn(instruction):
                    k[0] += 1
                    instruction.then_inc(g_bn, 1)
                    gp.wait_ge(g_bn, k[0])

                bn(gp.memset(mhalf[:], -0.5))
                bn(gp.tensor_scalar(bn_w[:, 0, :], par_s[:, :, 4], EPS, None, ALU.add))
                bn(gp.tensor_tensor(bn_w[:, 1, :], bn_w[:, 0, :], mhalf[:], ALU.pow))
                bn(gp.tensor_tensor(bn_w[:, 2, :], bn_w[:, 1, :], bn_w[:, 1, :], ALU.mult))
                bn(gp.tensor_tensor(bn_w[:, 2, :], bn_w[:, 2, :], bn_w[:, 0, :], ALU.mult))
                bn(gp.tensor_scalar(bn_w[:, 2, :], bn_w[:, 2, :], -0.5, 1.5, ALU.mult, ALU.add))
                bn(gp.tensor_tensor(bn_w[:, 1, :], bn_w[:, 1, :], bn_w[:, 2, :], ALU.mult))
                bn(gp.tensor_tensor(bn_s[:], bn_w[:, 1, :], par_s[:, :, 1], ALU.mult))
                bn(gp.tensor_tensor(bn_w[:, 3, :], par_s[:, :, 0], par_s[:, :, 3], ALU.subtract))
                bn(gp.tensor_tensor(bn_w[:, 3, :], bn_w[:, 3, :], bn_s[:], ALU.mult))
                bn(gp.tensor_tensor(bn_t[:], bn_w[:, 3, :], par_s[:, :, 2], ALU.add))
                bn(gp.tensor_scalar(nbd[:], wg_s[:, 12:13], -1.0, None, ALU.mult))
                done(gp.iota(iota_i[:], pattern=[[1, P]], base=0, channel_multiplier=0))
                done(gp.tensor_copy(iota_f[:], iota_i[:]))
                done(gp.iota(base_i[:], pattern=[[1, TAPS]], base=-1, channel_multiplier=1))
                done(gp.tensor_copy(base_f[:], base_i[:]))
                done(gp.memset(mask[:], NEG))
                taps = {(i * d, j * d) for d in (1, 2, 4) for i in (-1, 0, 1) for j in (-1, 0, 1)}
                for dr, dc in sorted(taps):
                    m = mask[:, :, HALO + dc:HALO + dc + SW, :]
                    done(gp.affine_select(out=m, in_=m, compare_op=ALU.not_equal,
                                          fill=LN3 if dr == dc == 0 else 0.0, base=SW * (HALO + dr),
                                          pattern=[[-SW * CROWS, 3], [-1, SW], [-SW, CROWS]],
                                          channel_multiplier=1))

            @block.vector
            def _(dve):
                nc.vector.memset(yp[:], 0.0).then_inc(v_zero, 1)
                dve.wait_ge(v_zero, 1)
                for u in range(UNITS):
                    last = nc.vector.memset(inside(yp, u, slice(0, 1)), 1.0)
                last.then_inc(v_zero, 1)
                nc.vector.memset(kh[:].bitcast(F32), 0.0)
                nc.vector.memset(kl[:].bitcast(F32), 0.0)
                nc.vector.memset(qq[:].bitcast(F32), 0.0)
                nc.vector.memset(v[:, :, :, HD:VCOLS], 1.0)
                nc.vector.memset(woT[:], 0.0).then_inc(v_zero, 1)
                dve.wait_ge(g_bn, 12)
                dve.wait_ge(in_w, 96)
                nc.vector.tensor_scalar(w1_s[:], w1_s[:], bn_s[:, 0:1], None, ALU.mult).then_inc(v_w, 1)
                nc.vector.tensor_scalar(w2_s[:, 0:HD], w2_s[:, 0:HD], bn_s[:, 1:2], None, ALU.mult).then_inc(v_w, 1)
                nc.vector.tensor_scalar(w2_s[:, HD:P], w2_s[:, HD:P], bn_s[:, 2:3], None, ALU.mult).then_inc(v_w, 1)
                dve.wait_ge(g_const, N_BAND)
                for k in range(TAPS):
                    nc.vector.tensor_scalar(conv[:, k, :], band[:, 0, :], wg_s[:, 3 * k:3 * k + 1], None,
                                            ALU.mult).then_inc(v_w, 1)
                for j in (1, 2):
                    dve.wait_ge(v_w, 3 + 3 * j)
                    for k in range(TAPS):
                        nc.vector.scalar_tensor_tensor(conv[:, k, :], band[:, j, :],
                                                       wg_s[:, 3 * k + j:3 * k + j + 1], conv[:, k, :],
                                                       ALU.mult, ALU.add).then_inc(v_w, 1)
                dve.wait_ge(t_w, 1)
                nc.vector.tensor_copy(w1T[:], ps_p[:, 0:P]).then_inc(v_tab, 1)
                nc.vector.tensor_copy(w2T[:], ps_p[:, P:2 * P]).then_inc(v_tab, 1)
                nc.vector.tensor_copy(wvT[:], ps_p[:, 2 * P:2 * P + HD]).then_inc(v_tab, 1)
                dve.wait_ge(v_zero, 3)
                nc.vector.tensor_copy(woT[0:HD, 0, :], ps_p[0:HD, 320:320 + P]).then_inc(v_tab, 1)
                nc.vector.tensor_copy(woT[HD:P, 1, :], ps_p[HD:P, 320:320 + P]).then_inc(v_tab, 1)
                dve.wait_ge(t_w, 2)
                for i, bank in enumerate((ps_t[0], ps_t[1], ps_c)):
                    nc.vector.tensor_copy(vbias[0:CKEYS, i, :, :].rearrange("p a b -> p (a b)"),
                                          bank[0:CKEYS, :]).then_inc(v_tab, 1)

            @block.tensor
            def _(pe):
                pe.wait_ge(g_const, N_ID)
                pe.wait_ge(v_w, 3)
                nc.tensor.transpose(ps_p[:, 0:P], w1_s[:], ident[:])
                nc.tensor.transpose(ps_p[:, P:2 * P], w2_s[:], ident[:])
                nc.tensor.transpose(ps_p[:, 2 * P:2 * P + HD], wv_s[:], ident[0:HD, 0:HD])
                nc.tensor.transpose(ps_p[:, 320:320 + P], wo_s[:], ident[:]).then_inc(t_w, 1)
                pe.wait_ge(v_zero, 2)
                for bank, c in ((ps_t[0], 0), (ps_t[1], 1), (ps_c, CHUNKS - 1)):
                    for s in range(STRIPS):
                        last = nc.tensor.matmul(bank[0:CKEYS, s * HD:(s + 1) * HD],
                                                window(yp, c, s, slice(0, 1)),
                                                bv_s[0:1, :], start=True, stop=True)
                last.then_inc(t_w, 1)

        events = []

        def event(name, per, step=1):
            events.append(Event(sem(name), per, step))
            return events[-1]

        x_in = [event("x_in0", 16, 2), event("x_in1", 16, 2)]
        stored = [event("stored0", 32), event("stored1", 32)]
        s_done = event("s_done", TILES)
        z_done = event("z_done", TILES)
        e_done = event("e_done", TILES)
        t_done = event("t_done", TILES)
        eT_done = event("eT_done", TILES)
        c_done = event("c_done", TILES)
        rd_done = event("rd_done", GROUPS)
        cx_done = event("cx_done", GROUPS)
        cT_ps = event("cT_ps", GROUPS)
        cT_done = event("cT_done", GROUPS)
        o_ps = event("o_ps", GROUPS)
        o_done = event("o_done", GROUPS)
        y_done = event("y_done", UNITS)
        x1_done = event("x1_done", UNITS)
        h_ps = event("h_ps", UNITS)
        h_done = event("h_done", UNITS)
        q_ps = event("q_ps", UNITS)
        tq_done = event("tq_done", UNITS)
        k_ps = event("k_ps", UNITS)
        tk_done = event("tk_done", UNITS)
        qh_done = event("qh_done", UNITS)
        ql_done = event("ql_done", UNITS)
        kh_done = event("kh_done", UNITS)
        kl_done = event("kl_done", UNITS)
        v_ps = event("v_ps", CHUNKS)
        v_done = event("v_done", CHUNKS)
        bs_done = event("bs_done", UNITS)
        dg, pg, cg, ag = event("dg", N_DG), event("pg", N_PG), event("cg", N_CG), event("ag", N_AG)

        def units_at(n, t):
            for m, rel in ((n, t), (n + 1, t - TILES)):
                if m.exists():
                    for u, at in enumerate(Y_SLOT):
                        if -1 <= rel - at <= 6:
                            yield m, u, rel - at

        def chain_at(n, t):
            for m, rel in ((n + 2, t), (n + 1, t + TILES)):
                if m.exists():
                    yield m, rel

        def query_tiles(u):
            b, half = divmod(u, 2)
            part = qq[:, STRIPS * b:STRIPS * (b + 1), UROWS * SW * half:UROWS * SW * (half + 1)]
            return part.rearrange("p s (r c) -> p r s c", c=SW)

        D, SQ, VE, R, T0, PL, POS, ZS, EX, GATE, RG, A_, M1, AV, D1, SQ1, VE1, R1, B_, YA, YB, M1G = (
            0, 1, 2, 3, 4, 5, 6, 9, 10, 11, 12, 13, 14, 15, 16, 17, 18, 19, 20, 21, 22, 23)
        X_A, X_B, Y_A, Y_B = 24, 26, 28, 30

        def col(c, n=1):
            return g1[:, c:c + n]

        def images(first, last, drain=0, register=None):
            with nc.Block() as block:
                @block.sync
                def _(sp):
                    def store(m, b):
                        rows = min(16, H - 16 * b)
                        sp.wait_ge(o_done.sem, o_done.count(m, 2 * b + 2))
                        sp.dma_start(out[m.index(), :, 16 * b * W:(16 * b + rows) * W],
                                     ost[:, b % 2, 0:rows, :].rearrange("p a b -> p (a b)")).then_inc(stored[b % 2].next(16), 16)

                    def slot(n, t):
                        if t == STORE + 3 * STRIPS - TILES and (n + -1).exists():
                            store(n + -1, 3)
                        m = n + 2
                        if t == 8 and m.exists():
                            if n.exists():
                                sp.wait_ge(x1_done.sem, x1_done.count(n, UNITS))
                                sp.wait_ge(y_done.sem, y_done.count(n, UNITS))
                            sp.dma_start(raw[:, m.parity(), :], x_d[m.index(), :, :]).then_inc(x_in[m.parity()].next(16), 16)
                        if t in range(STORE, TILES, STRIPS) and n.exists():
                            store(n, (t - STORE) // STRIPS)

                    for n, t in slots(first, last, drain, register):
                        slot(n, t)
                    for transfers in x_in + stored:
                        sp.wait_ge(transfers.sem, transfers.here)

                @block.tensor
                def _(pe):
                    def scores(n, t):
                        b, s, rows, _ = tile(t)
                        if t % STRIPS == 0:
                            pe.wait_ge(ql_done.sem, ql_done.count(n, BAND_UNITS[b]))
                            pe.wait_ge(kl_done.sem, kl_done.count(n, BAND_UNITS[b]))
                        pe.wait_ge(z_done.sem, z_done.count(n, t - 1))
                        chunks = window_chunks(t)
                        o = ps_s[t % 2][0:MAXQ, 0:len(chunks), :]

                        def keys(buf):
                            return buf[:].rearrange("p (c k) -> p c k", k=CPIX)[
                                :, chunks.start:chunks.stop, CROWS * SW * s:CROWS * SW * s + CKEYS]
                        nc.tensor.matmul(o, qq[:, t, :], keys(kh), start=True, stop=False)
                        nc.tensor.matmul(o, qq[0:HD, t, :], keys(kl), start=False,
                                         stop=True).then_inc(s_done.next(), 1)

                    def transposed(n, t):
                        _, _, rows, nq = tile(t)
                        pe.wait_ge(e_done.sem, e_done.count(n, t + 1))
                        pe.wait_ge(eT_done.sem, eT_done.count(n, t - 1))
                        for i in range(len(window_chunks(t))):
                            last = nc.tensor.transpose(ps_t[t % 2][0:CKEYS, i * nq:(i + 1) * nq],
                                                       e[0:nq, t % RING, i * CKEYS:(i + 1) * CKEYS], ident[0:nq, 0:nq])
                        last.then_inc(t_done.next(), 1)

                    def context(n, t):
                        b, s, _, nq = tile(t)
                        if t % STRIPS == 0:
                            pe.wait_ge(v_done.sem, v_done.count(n, BAND_CHUNKS[b]))
                        pe.wait_ge(eT_done.sem, eT_done.count(n, t + 1))
                        g, j = divmod(t, TPG)
                        pe.wait_ge(cx_done.sem, cx_done.count(n, g))
                        chunks = window_chunks(t)
                        for i, c in enumerate(chunks):
                            last = nc.tensor.matmul(ps_c[0:nq, j * VCOLS:(j + 1) * VCOLS],
                                                    eT[:, t % RING, i * nq:(i + 1) * nq], v[:, c, s, :],
                                                    start=(i == 0), stop=(i == len(chunks) - 1))
                        last.then_inc(c_done.next(), 1)

                    def context_transposed(n, g):
                        nq = tile(g * TPG)[3]
                        pe.wait_ge(cx_done.sem, cx_done.count(n, g + 1))
                        pe.wait_ge(o_done.sem, o_done.count(n, g))
                        for h in range(2):
                            last = nc.tensor.transpose(ps_g[:, h * nq:(h + 1) * nq],
                                                       cx[0:nq, 2 * h:2 * h + 2, :].rearrange("p a b -> p (a b)"),
                                                       ident[0:nq, 0:nq])
                        last.then_inc(cT_ps.next(), 1)

                    def output(n, g):
                        nq = tile(g * TPG)[3]
                        pe.wait_ge(cT_done.sem, cT_done.count(n, g + 1))
                        o = ps_g[:, 0:4 * nq].rearrange("p (h a q) -> p h a q", h=2, a=2)
                        for a in range(2):
                            last = nc.tensor.matmul(o[:, :, a, :], woT[:, a, :], cT[:, :, 0:nq], start=True, stop=True)
                        last.then_inc(o_ps.next(), 1)

                    def hidden(m, u):
                        pe.wait_ge(y_done.sem, y_done.count(m, u + 1))
                        pe.wait_ge(tk_done.sem, tk_done.count(m, u))
                        nc.tensor.matmul(ps_p[:, 0:UPIX], w1T[:], inside(yp, u), start=True,
                                         stop=True).then_inc(h_ps.next(), 1)

                    def query(m, u):
                        pe.wait_ge(h_done.sem, h_done.count(m, u + 1))
                        nc.tensor.matmul(ps_p[:, 0:UPIX], w2T[0:HD, :], hid[0:HD, :, :], start=True,
                                         stop=True).then_inc(q_ps.next(), 1)

                    def key(m, u):
                        pe.wait_ge(tq_done.sem, tq_done.count(m, u + 1))
                        nc.tensor.matmul(ps_p[:, 0:UPIX], w2T[HD:P, :], hid[HD:P, :, :], start=True,
                                         stop=True).then_inc(k_ps.next(), 1)

                    def values(m, c):
                        pe.wait_ge(y_done.sem, y_done.count(m, min(c + 1, UNITS)))
                        pe.wait_ge(v_done.sem, v_done.count(m, c))
                        if (m + 1).exists():
                            reads = [k for k, at in CHAIN_READS if CH[at] <= V_SLOT[c] + TILES]
                            pe.wait_ge(dg.sem, dg.count(m + 1, max(reads, default=0)))
                        for s in range(STRIPS):
                            last = nc.tensor.matmul(ps_v[0:CKEYS, s * HD:(s + 1) * HD], window(yp, c, s), wvT[:],
                                                    start=True, stop=True)
                        last.then_inc(v_ps.next(), 1)

                    def chain(m, at):
                        if at in (CH["c1"], CH["c2"], CH["c3"], CH["c4"], CH["c5"]):
                            chunks = sum(v_at < at - TILES for v_at in V_SLOT)
                            pe.wait_ge(v_done.sem, v_done.count(m + -1, chunks))

                        def avg(k, src, ready, to):
                            pe.wait_ge(dg.sem, dg.count(m, ready))
                            nc.tensor.matmul(ps_v[:, to:to + 1], group_avg[:], src, start=True,
                                             stop=True).then_inc(cg.next(), 1)
                        if at == CH["c1"]:
                            avg(1, st[:, 0:1], 1, 0)
                        if at == CH["c2"]:
                            avg(2, col(SQ), 3, 1)
                        if at == CH["c3"]:
                            pe.wait_ge(pg.sem, pg.count(m, 7))
                            for k in range(TAPS):
                                nc.tensor.matmul(ps_v[:, 4 + k:5 + k], conv[:, k, :], col(PL), start=True, stop=True)
                            nc.tensor.matmul(ps_v[:, 8:8 + P], ones[:], diag[:], start=True, stop=True).then_inc(cg.next(), 1)
                        if at == CH["c4"]:
                            pe.wait_ge(pg.sem, pg.count(m, 20))
                            nc.tensor.matmul(ps_v[:, 2:3], group_avg[:], col(M1), start=True, stop=True).then_inc(cg.next(), 1)
                        if at == CH["c5"]:
                            avg(5, col(SQ1), 12, 3)

                    def slot(n, t):
                        if n.exists():
                            scores(n, t)
                        for lag, work in ((TRANSPOSE, transposed), (CONTEXT, context)):
                            m, k = lagged(n, t, lag)
                            if m.exists():
                                work(m, k)
                        m, k = lagged(n, t, CX_TRANSPOSE)
                        if k % TPG == 0 and m.exists():
                            context_transposed(m, k // TPG)
                        m, k = lagged(n, t, OUTPUT)
                        if k % TPG == 0 and m.exists():
                            output(m, k // TPG)
                        for m, u, since in units_at(n, t):
                            if since == 1:
                                hidden(m, u)
                            if since == 2:
                                query(m, u)
                            if since == 3:
                                key(m, u)
                            if since == 4:
                                values(m, u)
                            if since == 5 and u == UNITS - 1:
                                values(m, u + 1)
                        for m, at in chain_at(n, t):
                            chain(m, at)

                    for n, t in slots(first, last, drain, register):
                        slot(n, t)

                @block.scalar
                def _(act):
                    def exponentials(n, t):
                        _, _, rows, nq = tile(t)
                        keys = (rows + CROWS) * WIN
                        act.wait_ge(z_done.sem, z_done.count(n, t + 1))
                        act.wait_ge(t_done.sem, t_done.count(n, t + 1 - RING))
                        nc.scalar.activation(e[0:nq, t % RING, 0:keys], z[0:nq, t % RING, 0:keys], ACT.Exp,
                                             bias=zmin[0:nq, t % RING:t % RING + 1], scale=-1.0).then_inc(e_done.next(), 1)

                    def copy(n, t):
                        _, _, _, nq = tile(t)
                        cols = nq * len(window_chunks(t))
                        act.wait_ge(t_done.sem, t_done.count(n, t + 1))
                        act.wait_ge(c_done.sem, c_done.count(n, t + 1 - RING))
                        nc.scalar.activation(eT[:, t % RING, 0:cols], ps_t[t % 2][0:CKEYS, 0:cols],
                                             ACT.Copy).then_inc(eT_done.next(), 1)

                    def relu(to, src, column):
                        return nc.scalar.activation(to, src, ACT.Relu, bias=bn_t[:, column:column + 1])

                    def slot(n, t):
                        m, k = lagged(n, t, TRANSPOSE)
                        if m.exists():
                            copy(m, k)
                        if n.exists():
                            exponentials(n, t)
                        for m, u, since in units_at(n, t):
                            flat = ps_p[:, 0:UPIX]
                            if since == 1:
                                act.wait_ge(h_ps.sem, h_ps.count(m, u + 1))
                                act.wait_ge(k_ps.sem, k_ps.count(m, u))
                                relu(hid[:].rearrange("p a b -> p (a b)"), flat, 0).then_inc(h_done.next(), 1)
                            if since == 2:
                                act.wait_ge(q_ps.sem, q_ps.count(m, u + 1))
                                act.wait_ge(ql_done.sem, ql_done.count(m, u))
                                relu(tq[:], flat, 1).then_inc(tq_done.next(), 1)
                            if since == 3:
                                act.wait_ge(k_ps.sem, k_ps.count(m, u + 1))
                                act.wait_ge(kl_done.sem, kl_done.count(m, u))
                                relu(tk[:], flat, 2).then_inc(tk_done.next(), 1)
                        for m, at in chain_at(n, t):
                            if at == CH["a4"]:
                                act.wait_ge(dg.sem, dg.count(m, 6))
                                act.wait_ge(pg.sem, pg.count((m + -1), 13))
                                for k in range(TAPS):
                                    nc.scalar.activation(hats[:, k, 0, :], iota_f[:], ACT.Abs, bias=col(POS + k),
                                                         scale=-1.0).then_inc(ag.next(), 1)
                            if at == CH["a6"]:
                                act.wait_ge(dg.sem, dg.count(m, 8))
                                nc.scalar.activation(col(EX), col(ZS), ACT.Exp, bias=nbd[:, 0:1],
                                                     scale=-1.0).then_inc(ag.next(), 1)

                    for n, t in slots(first, last, drain, register):
                        slot(n, t)

                @block.gpsimd
                def _(gp):
                    def chain(m, at):
                        def steps(first, *instructions):
                            for i, make in enumerate(instructions):
                                gp.wait_ge(pg.sem, pg.count(m, first + i))
                                make().then_inc(pg.next(), 1)

                        def rsqrt(to, ve, t):
                            return (lambda: gp.tensor_tensor(to, ve, mhalf[:, 0:1], ALU.pow),
                                    lambda: gp.tensor_tensor(t, to, to, ALU.mult),
                                    lambda: gp.tensor_tensor(t, t, ve, ALU.mult),
                                    lambda: gp.tensor_scalar(t, t, -0.5, 1.5, ALU.mult, ALU.add),
                                    lambda: gp.tensor_tensor(to, to, t, ALU.mult))
                        if at == CH["p3"]:
                            gp.wait_ge(dg.sem, dg.count(m, 4))
                            steps(0, *rsqrt(col(R), col(VE), col(T0)),
                                  lambda: gp.tensor_tensor(col(PL), col(D), col(R), ALU.mult),
                                  lambda: gp.tensor_scalar(diag[:], ident[:], col(PL), None, ALU.mult))
                        if at == CH["p4"]:
                            gp.wait_ge(ag.sem, ag.count(m, 3))

                            def tap(k):
                                far, hat = hats[:, k, 0, :], hats[:, k, 1, :]
                                return (lambda: gp.tensor_scalar(hat, far, -1.0, 1.0, ALU.mult, ALU.add),
                                        lambda: gp.tensor_scalar(hat, hat, 0.0, wg_s[:, 9 + k:10 + k], ALU.max, ALU.mult))
                            steps(7, *tap(0), *tap(1), *tap(2),
                                  lambda: gp.tensor_tensor(hat_sum[:], hats[:, 0, 1, :], hats[:, 1, 1, :], ALU.add),
                                  lambda: gp.tensor_tensor(hat_sum[:], hat_sum[:], hats[:, 2, 1, :], ALU.add))
                        if at == CH["p7"]:
                            gp.wait_ge(dg.sem, dg.count(m, 10))
                            steps(15,
                                  lambda: gp.tensor_tensor(col(RG), col(R), col(GATE), ALU.mult),
                                  lambda: gp.tensor_scalar(col(A_), col(RG), 1.0, None, ALU.add),
                                  lambda: gp.tensor_tensor(col(T0), col(RG), col(D), ALU.mult),
                                  lambda: gp.tensor_tensor(col(AV), col(A_), col(A_), ALU.mult),
                                  lambda: gp.tensor_tensor(col(M1), col(T0), st[:, 0:1], ALU.add),
                                  lambda: gp.tensor_tensor(col(AV), col(AV), st[:, 1:2], ALU.mult),
                                  lambda: gp.tensor_tensor(col(M1G), st[:, 0:1], col(D), ALU.subtract),
                                  lambda: gp.tensor_tensor(col(M1G), col(M1G), col(RG), ALU.mult))
                        if at == CH["p11"]:
                            gp.wait_ge(dg.sem, dg.count(m, 13))
                            gp.wait_ge(y_done.sem, y_done.count(m + -1, 0))
                            gp.wait_ge(x1_done.sem, x1_done.count(m + -1, 0))
                            steps(23, *rsqrt(col(R1), col(VE1), col(T0)),
                                  lambda: gp.tensor_tensor(col(YA), col(A_), col(R1), ALU.mult),
                                  lambda: gp.tensor_tensor(col(T0), col(D1), col(M1), ALU.subtract),
                                  lambda: gp.tensor_tensor(col(T0), col(T0), col(M1G), ALU.subtract),
                                  lambda: gp.tensor_tensor(col(YB), col(T0), col(R1), ALU.mult),
                                  lambda: gp.tensor_tensor(col(B_), bo_s[:], col(M1G), ALU.subtract),
                                  lambda: gp.tensor_scalar(col(X_A + m.parity()), col(A_), 1.0, None, ALU.mult),
                                  lambda: gp.tensor_scalar(col(X_B + m.parity()), col(B_), 1.0, None, ALU.mult),
                                  lambda: gp.tensor_scalar(col(Y_A + m.parity()), col(YA), 1.0, None, ALU.mult),
                                  lambda: gp.tensor_scalar(col(Y_B + m.parity()), col(YB), 1.0, None, ALU.mult))

                    def normed(m, u):
                        if u == 0:
                            gp.wait_ge(pg.sem, pg.count(m, N_PG))
                        gp.wait_ge(v_ps.sem, v_ps.count(m + -1, u + 2))
                        gp.tensor_scalar(inside(yp, u), halves(raw[:, m.parity(), UPIX * u:UPIX * (u + 1)]),
                                         col(Y_A + m.parity()), col(Y_B + m.parity()),
                                         ALU.mult, ALU.add).then_inc(y_done.next(), 1)

                    def residual(m, u):
                        gp.wait_ge(o_done.sem, o_done.count(m + -1, 2 * (u // 2) + 2))
                        gp.tensor_scalar(x1[:, UROWS * u:UROWS * (u + 1), :].rearrange("p a b -> p (a b)"),
                                         raw[:, m.parity(), UPIX * u:UPIX * (u + 1)],
                                         col(X_A + m.parity()), col(X_B + m.parity()),
                                         ALU.mult, ALU.add).then_inc(x1_done.next(), 1)

                    def slot(n, t):
                        for m, u, since in units_at(n, t):
                            if since == -1:
                                normed(m, u)
                            if since == 3:
                                residual(m, u)
                            if since == 5:
                                gp.wait_ge(kh_done.sem, kh_done.count(m, u + 1))
                                gp.tensor_tensor(inside(kl, u, slice(0, HD)), halves(tk[0:HD, :]),
                                                 inside(kh, u, slice(0, HD)).bitcast(F32),
                                                 ALU.subtract).then_inc(kl_done.next(), 1)
                                gp.wait_ge(kl_done.sem, kl_done.count(m, u + 1))
                        for m, at in chain_at(n, t):
                            chain(m, at)

                    for n, t in slots(first, last, drain, register):
                        slot(n, t)

                @block.vector
                def _(dve):
                    def masked(n, t):
                        _, _, rows, nq = tile(t)
                        chunks = len(window_chunks(t))
                        dve.wait_ge(s_done.sem, s_done.count(n, t + 1))
                        dve.wait_ge(e_done.sem, e_done.count(n, t + 1 - RING))
                        nc.vector.tensor_tensor_reduce(
                            z[0:nq, t % RING, 0:chunks * CKEYS],
                            ps_s[t % 2][0:nq, 0:chunks, :].rearrange("p c k -> p (c k)"),
                            mask[0:nq, 0:chunks].rearrange("p c a b -> p (c a b)"), scale=-1.0, scalar=3e38,
                            op0=ALU.add, op1=ALU.min, accum_out=zmin[0:nq, t % RING:t % RING + 1]).then_inc(z_done.next(), 1)

                    def normalised(n, g):
                        nq = tile(g * TPG)[3]
                        dve.wait_ge(c_done.sem, c_done.count(n, TPG * (g + 1)))
                        dve.wait_ge(cT_ps.sem, cT_ps.count(n, g))
                        c = ps_c[0:nq, 0:TPG * VCOLS].rearrange("p (a b) -> p a b", b=VCOLS)
                        nc.vector.reciprocal(rden[0:nq, :], c[:, :, HD]).then_inc(rd_done.next(), 1)
                        dve.wait_ge(rd_done.sem, rd_done.count(n, g + 1))
                        nc.vector.tensor_tensor(cx[0:nq, :, :], c[:, :, 0:HD],
                                                rden[0:nq, :].unsqueeze(2).to_broadcast([nq, TPG, HD]),
                                                ALU.mult).then_inc(cx_done.next(), 1)

                    def context_copy(n, g):
                        nq = tile(g * TPG)[3]
                        dve.wait_ge(cT_ps.sem, cT_ps.count(n, g + 1))
                        dve.wait_ge(o_ps.sem, o_ps.count(n, g))
                        nc.vector.tensor_copy(cT[:, :, 0:nq], ps_g[:, 0:2 * nq].rearrange("p (a b) -> p a b", a=2)
                                              ).then_inc(cT_done.next(), 1)

                    def final(n, g):
                        b, s, rows, nq = tile(g * TPG)
                        dve.wait_ge(o_ps.sem, o_ps.count(n, g + 1))
                        dve.wait_ge(stored[b % 2].sem, stored[b % 2].count(n, 16 * (b // 2)))

                        dve.wait_ge(x1_done.sem, x1_done.count(n, min(2 * b + 2, UNITS)))

                        def part(t):
                            return t[:, :, SW * s:SW * (s + TPG)].rearrange("p h (a w) -> p a h w", w=SW)
                        nc.vector.tensor_tensor(part(ost[:, b % 2, 0:rows, :]),
                                                ps_g[:, 0:TPG * nq].rearrange("p (a h w) -> p a h w", a=TPG, w=SW),
                                                part(x1[:, 16 * b:16 * b + rows, :]), ALU.add).then_inc(o_done.next(), 1)

                    def values_copy(m, c):
                        dve.wait_ge(v_ps.sem, v_ps.count(m, c + 1))
                        kind = 0 if c == 0 else 2 if c == CHUNKS - 1 else 1
                        nc.vector.tensor_tensor(v[:, c, :, 0:HD],
                                                ps_v[0:CKEYS, :].rearrange("p (a b) -> p a b", b=HD),
                                                vbias[0:CKEYS, kind, :, :], ALU.add).then_inc(v_done.next(), 1)

                    def chain(m, at):
                        def step(k, instruction):
                            instruction.then_inc(dg.next(), 1)
                            dve.wait_ge(dg.sem, dg.count(m, k))

                        i = at - CH["stats"]
                        if 0 <= i < UNITS:
                            if i == 0:
                                dve.wait_ge(x_in[m.parity()].sem, x_in[m.parity()].count(m, 16))
                                dve.wait_ge(dg.sem, dg.count(m, 0))
                            nc.vector.bn_stats(stats[:, i, :], raw[:, m.parity(), UPIX * i:UPIX * (i + 1)]
                                               ).then_inc(bs_done.next(), 1)
                        if at == CH["aggr"]:
                            dve.wait_ge(bs_done.sem, bs_done.count(m, UNITS))
                            step(1, nc.vector.bn_aggr(st[:], stats[:].rearrange("p a b -> p (a b)")))
                        if at == CH["d1"]:
                            dve.wait_ge(cg.sem, cg.count(m, 1))
                            step(2, nc.vector.tensor_tensor(col(D), st[:, 0:1], ps_v[:, 0:1], ALU.subtract))
                            step(3, nc.vector.scalar_tensor_tensor(col(SQ), col(D), col(D), st[:, 1:2],
                                                                   ALU.mult, ALU.add))
                        if at == CH["d3"]:
                            dve.wait_ge(cg.sem, cg.count(m, 2))
                            step(4, nc.vector.tensor_scalar(col(VE), ps_v[:, 1:2], EPS, None, ALU.add))
                        if at == CH["d4"]:
                            dve.wait_ge(cg.sem, cg.count(m, 3))
                            step(5, nc.vector.tensor_tensor(col(POS, 3), ps_v[:, 4:7], base_f[:], ALU.add))
                            step(6, nc.vector.tensor_scalar(col(POS, 3), col(POS, 3), 0.0, P - 1.0, ALU.max, ALU.min))
                            step(7, nc.vector.tensor_copy(pooled_row[:], ps_v[:, 8:8 + P]))
                        if at == CH["d6"]:
                            dve.wait_ge(pg.sem, pg.count(m, 15))
                            step(8, nc.vector.scalar_tensor_tensor(junk[:], pooled_row[:], 1.0, hat_sum[:],
                                                                   ALU.mult, ALU.mult, accum_out=col(ZS)))
                        if at == CH["d7"]:
                            dve.wait_ge(ag.sem, ag.count(m, 4))
                            step(9, nc.vector.tensor_scalar(col(EX), col(EX), 1.0, None, ALU.add))
                            step(10, nc.vector.reciprocal(col(GATE), col(EX)))
                        if at == CH["d9"]:
                            dve.wait_ge(cg.sem, cg.count(m, 4))
                            step(11, nc.vector.tensor_tensor(col(D1), col(M1), ps_v[:, 2:3], ALU.subtract))
                            dve.wait_ge(pg.sem, pg.count(m, 23))
                            step(12, nc.vector.scalar_tensor_tensor(col(SQ1), col(D1), col(D1), col(AV),
                                                                    ALU.mult, ALU.add))
                        if at == CH["d11"]:
                            dve.wait_ge(cg.sem, cg.count(m, 5))
                            step(13, nc.vector.tensor_scalar(col(VE1), ps_v[:, 3:4], EPS, None, ALU.add))

                    def slot(n, t):
                        if n.exists():
                            masked(n, t)
                        m, k = lagged(n, t, CT_COPY)
                        if k % TPG == 0 and m.exists():
                            context_copy(m, k // TPG)
                        m, k = lagged(n, t, FINAL)
                        if k % TPG == 0 and m.exists():
                            final(m, k // TPG)
                        for m, u, since in units_at(n, t):
                            if since == 3:
                                dve.wait_ge(tq_done.sem, tq_done.count(m, u + 1))
                                tiles = query_tiles(u)
                                src = tq[:].rearrange("p (r s c) -> p r s c", s=STRIPS, c=SW)
                                nc.vector.tensor_copy(tiles, src).then_inc(qh_done.next(), 1)
                                dve.wait_ge(qh_done.sem, qh_done.count(m, u + 1))
                                nc.vector.tensor_tensor(tiles[HD:P], src[HD:P], tiles[HD:P].bitcast(F32),
                                                        ALU.subtract).then_inc(ql_done.next(), 1)
                            if since == 4:
                                dve.wait_ge(tk_done.sem, tk_done.count(m, u + 1))
                                nc.vector.tensor_copy(inside(kh, u), halves(tk[:])).then_inc(kh_done.next(), 1)
                            if since == 5:
                                values_copy(m, u)
                            if since == 6 and u == UNITS - 1:
                                values_copy(m, u + 1)
                        for m, at in chain_at(n, t):
                            chain(m, at)
                        m, k = lagged(n, t, NORM)
                        if k % TPG == 0 and m.exists():
                            normalised(m, k // TPG)

                    for n, t in slots(first, last, drain, register):
                        slot(n, t)

        def restart(rounds=1):
            for e in events:
                e.end_part(rounds)
            with nc.Block() as block:
                @block.gpsimd
                def _(gp):
                    gp.sem_clear(range(events[0].sem.num, events[-1].sem.num + 1))

        images(-2, 1)
        restart()
        with nc.Fori(0, ROUNDS) as i:
            images(2, 1 + ROUND, register=i)
            restart(ROUNDS)
        images(NIMG - 2, NIMG - 1, drain=DRAIN)


def kernel(**inputs):
    import numpy as _np
    import concourse.bacc as _bacc
    from concourse import mybir as _mybir
    from concourse.bass_utils import run_bass_kernel_spmd as _run

    a = {k.replace("L1_conv_", "").replace("L0_conv_", ""): _np.asarray(v) for k, v in inputs.items()}
    x = a["x"]

    def stacked(top, bottom, layer):
        return _np.stack([_np.concatenate([a[f"{top}{layer}_{p}"], a[f"{bottom}{layer}_{p}"]])
                          for p in ("b", "g", "be", "m", "v")], axis=1)
    w2 = _np.concatenate([a["q2_w"], a["k2_w"]], axis=1)
    arrays = {
        "x": x.reshape(NIMG, P, H * W),
        "par": _np.concatenate([stacked("q", "k", 1), stacked("q", "q", 2), stacked("k", "k", 2)], axis=1),
        "w1": _np.concatenate([a["q1_w"], a["k1_w"]], axis=0),
        "w2": _np.concatenate([w2, w2], axis=0),
        "wv": a["v_w"],
        "wo": _np.concatenate([a["w_w"], a["w_w"]], axis=1),
        "bo": a["w_b"].reshape(P, 1),
        "bv": a["v_b"].reshape(1, HD),
        "wg": _np.concatenate([a["w_offset"].reshape(-1), a["w_deform"].reshape(-1), a["b_deform"].reshape(-1)]),
    }
    nc = _bacc.Bacc("TRN2", target_bir_lowering=False, num_devices=1)
    arrays = {f"in_{k}_dram": _np.ascontiguousarray(t) for k, t in arrays.items()}
    args = [nc.dram_tensor(k, t.shape, _mybir.dt.from_np(t.dtype), kind="ExternalInput").ap()
            for k, t in arrays.items()]
    args.append(nc.dram_tensor("out_0_dram", (NIMG, P, H * W), _mybir.dt.float32, kind="ExternalOutput").ap())
    build(nc, *args)
    r = _run(nc, [arrays], core_ids=[0])
    return r.results[0]["out_0_dram"].reshape(x.shape)
```

```python
from contextlib import ExitStack

import concourse.bass as bass
from concourse import mybir

F32 = mybir.dt.float32
F32R = mybir.dt.float32r
I32 = mybir.dt.int32
ALU = mybir.AluOpType
ACT = mybir.ActivationFunctionType

P = 128
NIMG = 32
ROUND = 4
ROUNDS = (NIMG - 4) // ROUND
H = W = 56
HALO = 4
HD = 64
UROWS = 8
UNITS = H // UROWS
UPIX = UROWS * W
PROWS = H + 2 * HALO
PCOLS = W + 2 * HALO
SW = 7
STRIPS = W // SW
WIN = SW + 2 * HALO
CROWS = 8
CHUNKS = PROWS // CROWS
CPIX = CROWS * PCOLS
CKEYS = CROWS * WIN
VCOLS = HD + 1
TILES = 4 * STRIPS
TPG = 4
GROUPS = TILES // TPG
MAXQ = 16 * SW
GN = 4
EPS = 1e-5
NEG = -1e30
LN3 = 1.0986122886681098
TAPS = 3


def tile(k):
    band, strip = divmod(k, STRIPS)
    rows = min(16, H - 16 * band)
    return band, strip, rows, rows * SW


def window_chunks(k):
    band, _, rows, _ = tile(k)
    return range(2 * band, 2 * band + (rows + 2 * HALO) // CROWS)


Y_SLOT = [-20, -16, -12, -8, -4, 0, 5]
V_SLOT = [at + 4 for at in Y_SLOT] + [10]
CHAIN_READS = ((2, "d1"), (4, "d3"), (7, "d4"), (11, "d9"), (13, "d11"))
BAND_UNITS = [3, 5, 7, 7]
BAND_CHUNKS = [3, 5, 7, 8]
CH = dict(stats=13, aggr=17, c1=18, d1=19, c2=22, d3=23, p3=24, c3=26, d4=27, a4=28, p4=28, d6=31,
          a6=32, d7=33, p7=33, c4=34, d9=35, p9=36, c5=38, d11=39, p11=39)
STATS_PER_SLOT = 2
TRANSPOSE, CONTEXT = 2, 4
NORM, CX_TRANSPOSE, CT_COPY, OUTPUT, FINAL = [TPG - 1 + CONTEXT + i for i in range(5)]
RING = 4
STORE = TPG + FINAL + 1
DRAIN = STORE + 3 * STRIPS - TILES + 1
N_DG, N_PG, N_CG, N_AG = 13, 33, 5, 4


class Image:

    def __init__(self, offset, register=None):
        self.offset, self.register = offset, register

    def __add__(self, n):
        return Image(self.offset + n, self.register)

    def exists(self):
        return self.register is not None or 0 <= self.offset < NIMG

    def parity(self):
        return self.offset % 2

    def index(self):
        return self.offset if self.register is None else self.register * ROUND + self.offset


class Event:

    def __init__(self, sem, per, step=1):
        self.sem, self.per, self.step = sem, per, step
        self.before, self.here = 0, 0

    def next(self, n=1):
        self.here += n
        return self.sem

    def count(self, m, k):
        return max(0, m.offset // self.step * self.per + k - self.before)

    def end_part(self, rounds):
        self.before += self.here * rounds
        self.here = 0


def lagged(n, t, lag):
    return (n, t - lag) if t >= lag else (n + -1, t - lag + TILES)


def slots(first, last, drain=0, register=None):
    for o in range(first, last + 1):
        for t in range(TILES):
            yield Image(o, register), t
    for t in range(drain):
        yield Image(last + 1, register), t


def build(nc, x, par, w1, w2, wv, wo, bo, bv, wg, out):
    x_d = x.rearrange("n c p -> n c p")
    with ExitStack() as ctx:
        def sb(name, shape, dt=F32):
            return ctx.enter_context(nc.sbuf_tensor(name, shape, dt))

        def sem(name):
            return ctx.enter_context(nc.semaphore(name))

        ident = sb("ident", [P, P])
        ones = sb("ones", [P, P])
        group_avg = sb("group_avg", [P, P])
        band = sb("band", [P, TAPS, P])
        conv = sb("conv", [P, TAPS, P])
        iota_i = sb("iota_i", [P, P], I32)
        iota_f = sb("iota_f", [P, P])
        base_i = sb("base_i", [P, TAPS], I32)
        base_f = sb("base_f", [P, TAPS])
        mhalf = sb("mhalf", [P, 2])
        mask = sb("mask", [P, 3, WIN, CROWS])
        par_s = sb("par_s", [P, 2, 5])
        bn_s = sb("bn_s", [P, 2])
        bn_t = sb("bn_t", [P, 2])
        bn_w = sb("bn_w", [P, 4, 2])
        w1_s = sb("w1_s", [P, P])
        w2_s = sb("w2_s", [P, P])
        wv_s = sb("wv_s", [P, P])
        wo_s = sb("wo_s", [P, P])
        bo_s = sb("bo_s", [P, 1])
        bv_s = sb("bv_s", [P, 1])
        wg_s = sb("wg_s", [P, 13])
        nbd = sb("nbd", [P, 1])
        w1T = sb("w1T", [P, P])
        w2T = sb("w2T", [P, P])
        wvT = sb("wvT", [P, P])
        woT = sb("woT", [P, 2, P])
        raw = sb("raw", [P, 2, H * W])
        x1 = sb("x1", [P, H, W])
        y = sb("y", [P, 2, UPIX])
        vT = sb("vT", [P, CHUNKS * CPIX])
        hid = sb("hid", [P, UPIX])
        tqk = sb("tqk", [P, UPIX])
        qq = sb("qq", [P, TILES, MAXQ], F32R)
        kh = sb("kh", [P, CHUNKS * CPIX], F32R)
        kl = sb("kl", [HD, CHUNKS * CPIX], F32R)
        v = sb("v", [CKEYS, CHUNKS, STRIPS, VCOLS])
        z = sb("z", [MAXQ, RING, 3 * CKEYS])
        zmin = sb("zmin", [MAXQ, RING])
        e = sb("e", [MAXQ, RING, 3 * CKEYS])
        eT = sb("eT", [CKEYS, RING, 3 * MAXQ])
        rden = sb("rden", [MAXQ, TPG])
        cx = sb("cx", [MAXQ, TPG, HD])
        cT = sb("cT", [P, 2, MAXQ])
        ost = sb("ost", [P, 2, 16, W])
        stats = sb("stats", [P, UNITS, 6])
        st = sb("st", [P, 2])
        g1 = sb("g1", [P, 48])
        hats = sb("hats", [P, TAPS, 2, P])
        hat_sum = sb("hat_sum", [P, P])
        diag = sb("diag", [P, P])
        pooled_row = sb("pooled_row", [P, P])
        junk = sb("junk", [P, P])

        ps_s = [ctx.enter_context(nc.psum_tensor(f"ps_s{i}", [P, 3, CKEYS], F32)) for i in range(2)]
        ps_t = [ctx.enter_context(nc.psum_tensor(f"ps_t{i}", [P, 512], F32)) for i in range(2)]
        ps_c = ctx.enter_context(nc.psum_tensor("ps_c", [P, 512], F32))
        ps_g = ctx.enter_context(nc.psum_tensor("ps_g", [P, 512], F32))
        ps_p = ctx.enter_context(nc.psum_tensor("ps_p", [P, 512], F32))
        ps_v = ctx.enter_context(nc.psum_tensor("ps_v", [P, 512], F32))

        def inside(buf, u, parts=slice(0, P), first=0, ahead=0):
            a = buf[parts, CPIX * u:CPIX * u + 1]
            return bass.AP(a.tensor, a.offset + CROWS * (HALO + first - ahead) + HALO,
                           [list(a.ap[0]), [CPIX - HALO, 2], [1, HALO], [CROWS, W - first]])

        def halves(a):
            return a.rearrange("p (h r c) -> p h r c", h=2, c=W)

        def window(buf, c, strip, parts=slice(0, P)):
            return buf[parts, CPIX * c + CROWS * SW * strip:CPIX * c + CROWS * SW * strip + CKEYS]

        in_par, in_w = sem("in_par"), sem("in_w")
        g_const = sem("g_const")
        g_bn = sem("g_bn")
        v_zero = sem("v_zero")
        v_w = sem("v_w")
        t_w = sem("t_w")
        v_tab = sem("v_tab")
        N_ID = 2
        N_BAND = N_ID + 1 + 3 + 4
        with nc.Block() as block:
            @block.sync
            def _(sp):
                sp.dma_start(par_s[:], par.rearrange("p (a b) -> p a b", a=2)).then_inc(in_par, 16)
                sp.dma_start(wg_s[:], wg.partition_broadcast(P)).then_inc(in_par, 16)
                sp.wait_ge(v_zero, 1)
                for s, d in ((w1_s[:], w1), (w2_s[0:HD, 0:HD], w2[0:HD, :]), (w2_s[HD:P, HD:P], w2[HD:P, :]), (wv_s[:], wv), (wo_s[:], wo), (bo_s[:], bo), (bv_s[:], bv)):
                    sp.dma_start(s, d).then_inc(in_w, 16)

            @block.gpsimd
            def _(gp):
                n = [0]

                def done(instruction):
                    n[0] += 1
                    instruction.then_inc(g_const, 1)
                    gp.wait_ge(g_const, n[0])

                done(gp.memset(ident[:], 0.0))
                done(gp.affine_select(out=ident[:], in_=ident[:], compare_op=ALU.not_equal, fill=1.0,
                                      base=0, pattern=[[-1, P]], channel_multiplier=1))
                done(gp.memset(ones[:], 1.0))
                g3 = group_avg[:].rearrange("p (a b) -> p a b", b=GN)
                done(gp.memset(group_avg[:], 1.0 / GN))
                done(gp.affine_select(out=g3, in_=g3, compare_op=ALU.is_ge, fill=0.0, base=0,
                                      pattern=[[-GN, P // GN], [0, GN]], channel_multiplier=1))
                done(gp.affine_select(out=g3, in_=g3, compare_op=ALU.is_ge, fill=0.0, base=GN - 1,
                                      pattern=[[GN, P // GN], [0, GN]], channel_multiplier=-1))
                done(gp.memset(band[:], 0.0))
                for j in range(TAPS):
                    done(gp.affine_select(out=band[:, j, :], in_=band[:, j, :], compare_op=ALU.not_equal,
                                          fill=1.0, base=1 - j, pattern=[[-1, P]], channel_multiplier=1))
                assert n[0] == N_BAND
                gp.wait_ge(in_par, 32)
                k = [0]

                def bn(instruction):
                    k[0] += 1
                    instruction.then_inc(g_bn, 1)
                    gp.wait_ge(g_bn, k[0])

                bn(gp.memset(mhalf[:], -0.5))
                bn(gp.tensor_scalar(bn_w[:, 0, :], par_s[:, :, 4], EPS, None, ALU.add))
                bn(gp.tensor_tensor(bn_w[:, 1, :], bn_w[:, 0, :], mhalf[:], ALU.pow))
                bn(gp.tensor_tensor(bn_w[:, 2, :], bn_w[:, 1, :], bn_w[:, 1, :], ALU.mult))
                bn(gp.tensor_tensor(bn_w[:, 2, :], bn_w[:, 2, :], bn_w[:, 0, :], ALU.mult))
                bn(gp.tensor_scalar(bn_w[:, 2, :], bn_w[:, 2, :], -0.5, 1.5, ALU.mult, ALU.add))
                bn(gp.tensor_tensor(bn_w[:, 1, :], bn_w[:, 1, :], bn_w[:, 2, :], ALU.mult))
                bn(gp.tensor_tensor(bn_s[:], bn_w[:, 1, :], par_s[:, :, 1], ALU.mult))
                bn(gp.tensor_tensor(bn_w[:, 3, :], par_s[:, :, 0], par_s[:, :, 3], ALU.subtract))
                bn(gp.tensor_tensor(bn_w[:, 3, :], bn_w[:, 3, :], bn_s[:], ALU.mult))
                bn(gp.tensor_tensor(bn_t[:], bn_w[:, 3, :], par_s[:, :, 2], ALU.add))
                bn(gp.tensor_scalar(nbd[:], wg_s[:, 12:13], -1.0, None, ALU.mult))
                done(gp.iota(iota_i[:], pattern=[[1, P]], base=0, channel_multiplier=0))
                done(gp.tensor_copy(iota_f[:], iota_i[:]))
                done(gp.iota(base_i[:], pattern=[[1, TAPS]], base=-1, channel_multiplier=1))
                done(gp.tensor_copy(base_f[:], base_i[:]))
                done(gp.memset(mask[:], NEG))
                taps = {(i * d, j * d) for d in (1, 2, 4) for i in (-1, 0, 1) for j in (-1, 0, 1)}
                for dr, dc in sorted(taps):
                    m = mask[:, :, HALO + dc:HALO + dc + SW, :]
                    done(gp.affine_select(out=m, in_=m, compare_op=ALU.not_equal,
                                          fill=LN3 if dr == dc == 0 else 0.0, base=SW * (HALO + dr),
                                          pattern=[[-SW * CROWS, 3], [-1, SW], [-SW, CROWS]],
                                          channel_multiplier=1))

            @block.vector
            def _(dve):
                nc.vector.memset(w2_s[:], 0.0).then_inc(v_zero, 1)
                nc.vector.memset(vT[:], 0.0)
                nc.vector.memset(kh[:].bitcast(F32), 0.0)
                nc.vector.memset(kl[:].bitcast(F32), 0.0)
                nc.vector.memset(qq[:].bitcast(F32), 0.0)
                nc.vector.memset(v[:, :, :, HD:VCOLS], 1.0)
                nc.vector.memset(woT[:], 0.0).then_inc(v_zero, 1)
                dve.wait_ge(g_bn, 12)
                dve.wait_ge(in_w, 7 * 16)
                nc.vector.tensor_scalar(w1_s[:], w1_s[:], bn_s[:, 0:1], None, ALU.mult).then_inc(v_w, 1)
                nc.vector.tensor_scalar(w2_s[:], w2_s[:], bn_s[:, 1:2], None, ALU.mult).then_inc(v_w, 1)
                dve.wait_ge(g_const, N_BAND)
                for k in range(TAPS):
                    nc.vector.tensor_scalar(conv[:, k, :], band[:, 0, :], wg_s[:, 3 * k:3 * k + 1], None,
                                            ALU.mult).then_inc(v_w, 1)
                for j in (1, 2):
                    dve.wait_ge(v_w, 2 + 3 * j)
                    for k in range(TAPS):
                        nc.vector.scalar_tensor_tensor(conv[:, k, :], band[:, j, :],
                                                       wg_s[:, 3 * k + j:3 * k + j + 1], conv[:, k, :],
                                                       ALU.mult, ALU.add).then_inc(v_w, 1)
                dve.wait_ge(t_w, 1)
                nc.vector.tensor_copy(w1T[:], ps_p[:, 0:P]).then_inc(v_tab, 1)
                nc.vector.tensor_copy(w2T[:], ps_p[:, P:2 * P]).then_inc(v_tab, 1)
                nc.vector.tensor_copy(wvT[:], ps_p[:, 2 * P:3 * P]).then_inc(v_tab, 1)
                dve.wait_ge(v_zero, 2)
                nc.vector.tensor_copy(woT[0:HD, 0, :], ps_p[0:HD, 3 * P:4 * P]).then_inc(v_tab, 1)
                nc.vector.tensor_copy(woT[HD:P, 1, :], ps_p[HD:P, 3 * P:4 * P]).then_inc(v_tab, 1)

            @block.tensor
            def _(pe):
                pe.wait_ge(g_const, N_ID)
                pe.wait_ge(v_w, 2)
                nc.tensor.transpose(ps_p[:, 0:P], w1_s[:], ident[:])
                nc.tensor.transpose(ps_p[:, P:2 * P], w2_s[:], ident[:])
                nc.tensor.transpose(ps_p[:, 2 * P:3 * P], wv_s[:], ident[:])
                nc.tensor.transpose(ps_p[:, 3 * P:4 * P], wo_s[:], ident[:]).then_inc(t_w, 1)

        events = []

        def event(name, per, step=1):
            events.append(Event(sem(name), per, step))
            return events[-1]

        x_in = [event("x_in0", 16, 2), event("x_in1", 16, 2)]
        stored = [event("stored0", 32), event("stored1", 32)]
        s_done = event("s_done", TILES)
        z_done = event("z_done", TILES)
        e_done = event("e_done", TILES)
        t_done = event("t_done", TILES)
        eT_done = event("eT_done", TILES)
        c_done = event("c_done", TILES)
        rd_done = event("rd_done", GROUPS)
        cx_done = event("cx_done", GROUPS)
        cT_ps = event("cT_ps", GROUPS)
        cT_done = event("cT_done", GROUPS)
        o_ps = event("o_ps", GROUPS)
        o_done = event("o_done", GROUPS)
        y_done = event("y_done", UNITS)
        x1_done = event("x1_done", UNITS)
        h_ps = event("h_ps", UNITS)
        h_done = event("h_done", UNITS)
        qk_ps = event("qk_ps", UNITS)
        qk_done = event("qk_done", UNITS)
        vT_ps = event("vT_ps", UNITS)
        vT_done = event("vT_done", UNITS)
        qh_done = event("qh_done", UNITS)
        ql_done = event("ql_done", UNITS)
        kh_done = event("kh_done", UNITS)
        kh2_done = event("kh2_done", UNITS)
        kl_done = event("kl_done", UNITS)
        v_ps = event("v_ps", CHUNKS)
        v_done = event("v_done", CHUNKS)
        bs_done = event("bs_done", UNITS)
        dg, pg, cg, ag = event("dg", N_DG), event("pg", N_PG), event("cg", N_CG), event("ag", N_AG)

        def units_at(n, t):
            for m, rel in ((n, t), (n + 1, t - TILES)):
                if m.exists():
                    for u, at in enumerate(Y_SLOT):
                        if -1 <= rel - at <= 6:
                            yield m, u, rel - at

        def chain_at(n, t):
            for m, rel in ((n + 2, t), (n + 1, t + TILES)):
                if m.exists():
                    yield m, rel

        def query_tiles(u):
            b, half = divmod(u, 2)
            part = qq[:, STRIPS * b:STRIPS * (b + 1), UROWS * SW * half:UROWS * SW * (half + 1)]
            return part.rearrange("p s (r c) -> p r s c", c=SW)

        D, SQ, VE, R, T0, PL, POS, ZS, EX, GATE, RG, M1, AV, D1, SQ1, VE1, R1, BM, M1G = (
            0, 1, 2, 3, 4, 5, 6, 9, 10, 11, 12, 13, 14, 15, 16, 17, 18, 19, 20)
        X_A, X_B, Y_A, Y_B = 24, 26, 28, 30

        def col(c, n=1):
            return g1[:, c:c + n]

        def images(first, last, drain=0, register=None):
            with nc.Block() as block:
                @block.sync
                def _(sp):
                    def store(m, b):
                        rows = min(16, H - 16 * b)
                        sp.wait_ge(o_done.sem, o_done.count(m, 2 * b + 2))
                        sp.dma_start(out[m.index(), :, 16 * b * W:(16 * b + rows) * W],
                                     ost[:, b % 2, 0:rows, :].rearrange("p a b -> p (a b)")).then_inc(stored[b % 2].next(16), 16)

                    def slot(n, t):
                        m = n + 2
                        if t == 9 and m.exists():
                            if n.exists():
                                sp.wait_ge(x1_done.sem, x1_done.count(n, UNITS))
                                sp.wait_ge(y_done.sem, y_done.count(n, UNITS))
                            sp.dma_start(raw[:, m.parity(), :], x_d[m.index(), :, :]).then_inc(x_in[m.parity()].next(16), 16)
                        band, at = divmod((t - STORE) % TILES, STRIPS)
                        m = n if t >= STORE else n + -1
                        if at == 0 and m.exists():
                            store(m, band)

                    for n, t in slots(first, last, drain, register):
                        slot(n, t)
                    for transfers in x_in + stored:
                        sp.wait_ge(transfers.sem, transfers.here)

                @block.tensor
                def _(pe):
                    def scores(n, t):
                        b, s, rows, _ = tile(t)
                        if t % STRIPS == 0:
                            pe.wait_ge(ql_done.sem, ql_done.count(n, BAND_UNITS[b]))
                            pe.wait_ge(kl_done.sem, kl_done.count(n, BAND_UNITS[b]))
                            pe.wait_ge(kh2_done.sem, kh2_done.count(n, BAND_UNITS[b]))
                        pe.wait_ge(z_done.sem, z_done.count(n, t - 1))
                        chunks = window_chunks(t)
                        o = ps_s[t % 2][0:MAXQ, 0:len(chunks), :]

                        def keys(buf):
                            return buf[:].rearrange("p (c k) -> p c k", k=CPIX)[
                                :, chunks.start:chunks.stop, CROWS * SW * s:CROWS * SW * s + CKEYS]
                        nc.tensor.matmul(o, qq[:, t, :], keys(kh), start=True, stop=False)
                        nc.tensor.matmul(o, qq[0:HD, t, :], keys(kl), start=False,
                                         stop=True).then_inc(s_done.next(), 1)

                    def transposed(n, t):
                        _, _, rows, nq = tile(t)
                        pe.wait_ge(e_done.sem, e_done.count(n, t + 1))
                        pe.wait_ge(eT_done.sem, eT_done.count(n, t - 1))
                        for i in range(len(window_chunks(t))):
                            last = nc.tensor.transpose(ps_t[t % 2][0:CKEYS, i * nq:(i + 1) * nq],
                                                       e[0:nq, t % RING, i * CKEYS:(i + 1) * CKEYS], ident[0:nq, 0:nq])
                        last.then_inc(t_done.next(), 1)

                    def context(n, t):
                        b, s, _, nq = tile(t)
                        if t % STRIPS == 0:
                            pe.wait_ge(v_done.sem, v_done.count(n, BAND_CHUNKS[b]))
                        pe.wait_ge(eT_done.sem, eT_done.count(n, t + 1))
                        g, j = divmod(t, TPG)
                        pe.wait_ge(cx_done.sem, cx_done.count(n, g))
                        chunks = window_chunks(t)
                        for i, c in enumerate(chunks):
                            last = nc.tensor.matmul(ps_c[0:nq, j * VCOLS:(j + 1) * VCOLS],
                                                    eT[:, t % RING, i * nq:(i + 1) * nq], v[:, c, s, :],
                                                    start=(i == 0), stop=(i == len(chunks) - 1))
                        last.then_inc(c_done.next(), 1)

                    def context_transposed(n, g):
                        nq = tile(g * TPG)[3]
                        pe.wait_ge(cx_done.sem, cx_done.count(n, g + 1))
                        pe.wait_ge(o_done.sem, o_done.count(n, g))
                        for h in range(2):
                            last = nc.tensor.transpose(ps_g[:, h * nq:(h + 1) * nq],
                                                       cx[0:nq, 2 * h:2 * h + 2, :].rearrange("p a b -> p (a b)"),
                                                       ident[0:nq, 0:nq])
                        last.then_inc(cT_ps.next(), 1)

                    def output(n, g):
                        nq = tile(g * TPG)[3]
                        pe.wait_ge(cT_done.sem, cT_done.count(n, g + 1))
                        o = ps_g[:, 0:4 * nq].rearrange("p (h a q) -> p h a q", h=2, a=2)
                        for a in range(2):
                            last = nc.tensor.matmul(o[:, :, a, :], woT[:, a, :], cT[:, :, 0:nq], start=True, stop=True)
                        last.then_inc(o_ps.next(), 1)

                    def hidden(m, u):
                        pe.wait_ge(y_done.sem, y_done.count(m, u + 1))
                        pe.wait_ge(qk_done.sem, qk_done.count(m, u))
                        nc.tensor.matmul(ps_p[:, 0:UPIX], w1T[:], y[:, (m.parity() + u) % 2, :], start=True,
                                         stop=True).then_inc(h_ps.next(), 1)

                    def value_projection(m, u):
                        pe.wait_ge(h_done.sem, h_done.count(m, u + 1))
                        nc.tensor.matmul(ps_p[:, 0:UPIX], wvT[:], y[:, (m.parity() + u) % 2, :], start=True,
                                         stop=True).then_inc(vT_ps.next(), 1)

                    def query_and_key(m, u):
                        pe.wait_ge(vT_done.sem, vT_done.count(m, u + 1))
                        nc.tensor.matmul(ps_p[:, 0:UPIX], w2T[:], hid[:], start=True,
                                         stop=True).then_inc(qk_ps.next(), 1)

                    def values(m, c):
                        pe.wait_ge(vT_done.sem, vT_done.count(m, min(c + 1, UNITS)))
                        pe.wait_ge(v_done.sem, v_done.count(m, c))
                        if (m + 1).exists():
                            reads = [k for k, at in CHAIN_READS if CH[at] <= V_SLOT[c] + TILES]
                            pe.wait_ge(dg.sem, dg.count(m + 1, max(reads, default=0)))
                        for s in range(0, STRIPS, 2):
                            last = nc.tensor.transpose(ps_v[0:CKEYS, s * HD:(s + 2) * HD], window(vT, c, s), ident[:])
                        last.then_inc(v_ps.next(), 1)

                    def chain(m, at):
                        if at in (CH["c1"], CH["c2"], CH["c3"], CH["c4"], CH["c5"]):
                            chunks = sum(v_at < at - TILES for v_at in V_SLOT)
                            pe.wait_ge(v_done.sem, v_done.count(m + -1, chunks))

                        def avg(k, src, ready, to):
                            pe.wait_ge(dg.sem, dg.count(m, ready))
                            nc.tensor.matmul(ps_v[:, to:to + 1], group_avg[:], src, start=True,
                                             stop=True).then_inc(cg.next(), 1)
                        if at == CH["c1"]:
                            avg(1, st[:, 0:1], 1, 0)
                        if at == CH["c2"]:
                            avg(2, col(SQ), 3, 1)
                        if at == CH["c3"]:
                            pe.wait_ge(pg.sem, pg.count(m, 7))
                            for k in range(TAPS):
                                nc.tensor.matmul(ps_v[:, 4 + k:5 + k], conv[:, k, :], col(PL), start=True, stop=True)
                            nc.tensor.matmul(ps_v[:, 8:8 + P], ones[:], diag[:], start=True, stop=True).then_inc(cg.next(), 1)
                        if at == CH["c4"]:
                            pe.wait_ge(pg.sem, pg.count(m, 20))
                            nc.tensor.matmul(ps_v[:, 2:3], group_avg[:], col(M1), start=True, stop=True).then_inc(cg.next(), 1)
                        if at == CH["c5"]:
                            avg(5, col(SQ1), 12, 3)

                    def slot(n, t):
                        if n.exists():
                            scores(n, t)
                        for lag, work in ((TRANSPOSE, transposed), (CONTEXT, context)):
                            m, k = lagged(n, t, lag)
                            if m.exists():
                                work(m, k)
                        m, k = lagged(n, t, CX_TRANSPOSE)
                        if k % TPG == 0 and m.exists():
                            context_transposed(m, k // TPG)
                        m, k = lagged(n, t, OUTPUT)
                        if k % TPG == 0 and m.exists():
                            output(m, k // TPG)
                        for m, u, since in units_at(n, t):
                            if since == 1:
                                hidden(m, u)
                            if since == 2:
                                value_projection(m, u)
                            if since == 3:
                                query_and_key(m, u)
                            if since == 4:
                                values(m, u)
                            if since == 5 and u == UNITS - 1:
                                values(m, u + 1)
                        for m, at in chain_at(n, t):
                            chain(m, at)

                    for n, t in slots(first, last, drain, register):
                        slot(n, t)

                @block.scalar
                def _(act):
                    def exponentials(n, t):
                        _, _, rows, nq = tile(t)
                        keys = (rows + CROWS) * WIN
                        act.wait_ge(z_done.sem, z_done.count(n, t + 1))
                        act.wait_ge(t_done.sem, t_done.count(n, t + 1 - RING))
                        nc.scalar.activation(e[0:nq, t % RING, 0:keys], z[0:nq, t % RING, 0:keys], ACT.Exp,
                                             bias=zmin[0:nq, t % RING:t % RING + 1], scale=-1.0).then_inc(e_done.next(), 1)

                    def copy(n, t):
                        _, _, _, nq = tile(t)
                        cols = nq * len(window_chunks(t))
                        act.wait_ge(t_done.sem, t_done.count(n, t + 1))
                        act.wait_ge(c_done.sem, c_done.count(n, t + 1 - RING))
                        nc.scalar.activation(eT[:, t % RING, 0:cols], ps_t[t % 2][0:CKEYS, 0:cols],
                                             ACT.Copy).then_inc(eT_done.next(), 1)

                    def relu(to, src, column):
                        return nc.scalar.activation(to, src, ACT.Relu, bias=bn_t[:, column:column + 1])

                    def slot(n, t):
                        m, k = lagged(n, t, TRANSPOSE)
                        if m.exists():
                            copy(m, k)
                        if n.exists():
                            exponentials(n, t)
                        for m, u, since in units_at(n, t):
                            flat = ps_p[:, 0:UPIX]
                            if since == 1:
                                act.wait_ge(h_ps.sem, h_ps.count(m, u + 1))
                                act.wait_ge(qk_ps.sem, qk_ps.count(m, u))
                                relu(hid[:], flat, 0).then_inc(h_done.next(), 1)
                            if since == 2:
                                act.wait_ge(vT_ps.sem, vT_ps.count(m, u + 1))
                                act.wait_ge(v_ps.sem, v_ps.count(m + -1, u + 2))
                                nc.scalar.activation(inside(vT, u, slice(0, HD)), halves(flat[0:HD]),
                                                     ACT.Identity, bias=bv_s[0:HD, 0:1])
                                first = SW - HALO
                                nc.scalar.activation(inside(vT, u, slice(HD, P), first, SW),
                                                     halves(flat[HD:P])[:, :, :, first:W],
                                                     ACT.Identity, bias=bv_s[HD:P, 0:1]).then_inc(vT_done.next(), 1)
                            if since == 3:
                                act.wait_ge(qk_ps.sem, qk_ps.count(m, u + 1))
                                act.wait_ge(ql_done.sem, ql_done.count(m, u))
                                act.wait_ge(kl_done.sem, kl_done.count(m, u))
                                relu(tqk[:], flat, 1).then_inc(qk_done.next(), 1)
                        for m, at in chain_at(n, t):
                            if at == CH["a4"]:
                                act.wait_ge(dg.sem, dg.count(m, 6))
                                act.wait_ge(pg.sem, pg.count((m + -1), 13))
                                for k in range(TAPS):
                                    nc.scalar.activation(hats[:, k, 0, :], iota_f[:], ACT.Abs, bias=col(POS + k),
                                                         scale=-1.0).then_inc(ag.next(), 1)
                            if at == CH["a6"]:
                                act.wait_ge(dg.sem, dg.count(m, 8))
                                nc.scalar.activation(col(EX), col(ZS), ACT.Exp, bias=nbd[:, 0:1],
                                                     scale=-1.0).then_inc(ag.next(), 1)

                    for n, t in slots(first, last, drain, register):
                        slot(n, t)

                @block.gpsimd
                def _(gp):
                    def chain(m, at):
                        def steps(first, *instructions):
                            for i, make in enumerate(instructions):
                                gp.wait_ge(pg.sem, pg.count(m, first + i))
                                make().then_inc(pg.next(), 1)

                        def rsqrt(to, ve, t):
                            return (lambda: gp.tensor_tensor(to, ve, mhalf[:, 0:1], ALU.pow),
                                    lambda: gp.tensor_tensor(t, to, to, ALU.mult),
                                    lambda: gp.tensor_tensor(t, t, ve, ALU.mult),
                                    lambda: gp.tensor_scalar(t, t, -0.5, 1.5, ALU.mult, ALU.add),
                                    lambda: gp.tensor_tensor(to, to, t, ALU.mult))
                        if at == CH["p3"]:
                            gp.wait_ge(dg.sem, dg.count(m, 4))
                            steps(0, *rsqrt(col(R), col(VE), col(T0)),
                                  lambda: gp.tensor_tensor(col(PL), col(D), col(R), ALU.mult),
                                  lambda: gp.tensor_scalar(diag[:], ident[:], col(PL), None, ALU.mult))
                        if at == CH["p4"]:
                            gp.wait_ge(ag.sem, ag.count(m, 3))

                            def tap(k):
                                far, hat = hats[:, k, 0, :], hats[:, k, 1, :]
                                return (lambda: gp.tensor_scalar(hat, far, -1.0, 1.0, ALU.mult, ALU.add),
                                        lambda: gp.tensor_scalar(hat, hat, 0.0, wg_s[:, 9 + k:10 + k], ALU.max, ALU.mult))
                            steps(7, *tap(0), *tap(1), *tap(2),
                                  lambda: gp.tensor_tensor(hat_sum[:], hats[:, 0, 1, :], hats[:, 1, 1, :], ALU.add),
                                  lambda: gp.tensor_tensor(hat_sum[:], hat_sum[:], hats[:, 2, 1, :], ALU.add))
                        if at == CH["p7"]:
                            gp.wait_ge(dg.sem, dg.count(m, 10))
                            gp.wait_ge(y_done.sem, y_done.count(m + -1, 0))
                            gp.wait_ge(x1_done.sem, x1_done.count(m + -1, 0))
                            a = col(X_A + m.parity())
                            steps(15,
                                  lambda: gp.tensor_tensor(col(RG), col(R), col(GATE), ALU.mult),
                                  lambda: gp.tensor_scalar(a, col(RG), 1.0, None, ALU.add),
                                  lambda: gp.tensor_tensor(col(T0), col(RG), col(D), ALU.mult),
                                  lambda: gp.tensor_tensor(col(AV), a, a, ALU.mult),
                                  lambda: gp.tensor_tensor(col(M1), col(T0), st[:, 0:1], ALU.add),
                                  lambda: gp.tensor_tensor(col(AV), col(AV), st[:, 1:2], ALU.mult),
                                  lambda: gp.tensor_tensor(col(M1G), st[:, 0:1], col(D), ALU.subtract),
                                  lambda: gp.tensor_tensor(col(M1G), col(M1G), col(RG), ALU.mult))
                        if at == CH["p9"]:
                            gp.wait_ge(dg.sem, dg.count(m, 11))
                            steps(23,
                                  lambda: gp.tensor_tensor(col(BM), col(D1), col(M1), ALU.subtract),
                                  lambda: gp.tensor_tensor(col(BM), col(BM), col(M1G), ALU.subtract),
                                  lambda: gp.tensor_tensor(col(X_B + m.parity()), bo_s[:], col(M1G), ALU.subtract))
                        if at == CH["p11"]:
                            gp.wait_ge(dg.sem, dg.count(m, 13))
                            steps(26, *rsqrt(col(R1), col(VE1), col(T0)),
                                  lambda: gp.tensor_tensor(col(Y_A + m.parity()), col(X_A + m.parity()), col(R1),
                                                           ALU.mult),
                                  lambda: gp.tensor_tensor(col(Y_B + m.parity()), col(BM), col(R1), ALU.mult))

                    def normed(m, u):
                        if u == 0:
                            gp.wait_ge(pg.sem, pg.count(m, N_PG))
                        gp.wait_ge(vT_ps.sem, vT_ps.count(m, u - 1))
                        gp.tensor_scalar(y[:, (m.parity() + u) % 2, :], raw[:, m.parity(), UPIX * u:UPIX * (u + 1)],
                                         col(Y_A + m.parity()), col(Y_B + m.parity()),
                                         ALU.mult, ALU.add).then_inc(y_done.next(), 1)

                    def residual(m, u):
                        gp.wait_ge(o_done.sem, o_done.count(m + -1, 2 * (u // 2) + 2))
                        gp.tensor_scalar(x1[:, UROWS * u:UROWS * (u + 1), :].rearrange("p a b -> p (a b)"),
                                         raw[:, m.parity(), UPIX * u:UPIX * (u + 1)],
                                         col(X_A + m.parity()), col(X_B + m.parity()),
                                         ALU.mult, ALU.add).then_inc(x1_done.next(), 1)

                    def slot(n, t):
                        for m, u, since in units_at(n, t):
                            if since == -1:
                                normed(m, u)
                            if since == 4:
                                residual(m, u)
                            if since == 4:
                                gp.wait_ge(qk_done.sem, qk_done.count(m, u + 1))
                                gp.wait_ge(y_done.sem, y_done.here)
                                gp.wait_ge(x1_done.sem, x1_done.here)
                                gp.wait_ge(pg.sem, pg.here)
                                gp.tensor_scalar(inside(kh, u, slice(HD, P)), halves(tqk[HD:P, :]), 1.0, None,
                                                 ALU.mult).then_inc(kh_done.next(), 1)
                                gp.wait_ge(kh_done.sem, kh_done.count(m, u + 1))
                        for m, at in chain_at(n, t):
                            chain(m, at)

                    for n, t in slots(first, last, drain, register):
                        slot(n, t)

                @block.vector
                def _(dve):
                    def masked(n, t):
                        _, _, rows, nq = tile(t)
                        chunks = len(window_chunks(t))
                        dve.wait_ge(s_done.sem, s_done.count(n, t + 1))
                        dve.wait_ge(e_done.sem, e_done.count(n, t + 1 - RING))
                        nc.vector.tensor_tensor_reduce(
                            z[0:nq, t % RING, 0:chunks * CKEYS],
                            ps_s[t % 2][0:nq, 0:chunks, :].rearrange("p c k -> p (c k)"),
                            mask[0:nq, 0:chunks].rearrange("p c a b -> p (c a b)"), scale=-1.0, scalar=3e38,
                            op0=ALU.add, op1=ALU.min, accum_out=zmin[0:nq, t % RING:t % RING + 1]).then_inc(z_done.next(), 1)

                    def normalised(n, g):
                        nq = tile(g * TPG)[3]
                        dve.wait_ge(c_done.sem, c_done.count(n, TPG * (g + 1)))
                        dve.wait_ge(cT_ps.sem, cT_ps.count(n, g))
                        c = ps_c[0:nq, 0:TPG * VCOLS].rearrange("p (a b) -> p a b", b=VCOLS)
                        nc.vector.reciprocal(rden[0:nq, :], c[:, :, HD]).then_inc(rd_done.next(), 1)
                        dve.wait_ge(rd_done.sem, rd_done.count(n, g + 1))
                        nc.vector.tensor_tensor(cx[0:nq, :, :], c[:, :, 0:HD],
                                                rden[0:nq, :].unsqueeze(2).to_broadcast([nq, TPG, HD]),
                                                ALU.mult).then_inc(cx_done.next(), 1)

                    def context_copy(n, g):
                        nq = tile(g * TPG)[3]
                        dve.wait_ge(cT_ps.sem, cT_ps.count(n, g + 1))
                        dve.wait_ge(o_ps.sem, o_ps.count(n, g))
                        nc.vector.tensor_copy(cT[:, :, 0:nq], ps_g[:, 0:2 * nq].rearrange("p (a b) -> p a b", a=2)
                                              ).then_inc(cT_done.next(), 1)

                    def final(n, g):
                        b, s, rows, nq = tile(g * TPG)
                        dve.wait_ge(o_ps.sem, o_ps.count(n, g + 1))
                        dve.wait_ge(stored[b % 2].sem, stored[b % 2].count(n, 16 * (b // 2)))

                        dve.wait_ge(x1_done.sem, x1_done.count(n, min(2 * b + 2, UNITS)))

                        def part(t):
                            return t[:, :, SW * s:SW * (s + TPG)].rearrange("p h (a w) -> p a h w", w=SW)
                        nc.vector.tensor_tensor(part(ost[:, b % 2, 0:rows, :]),
                                                ps_g[:, 0:TPG * nq].rearrange("p (a h w) -> p a h w", a=TPG, w=SW),
                                                part(x1[:, 16 * b:16 * b + rows, :]), ALU.add).then_inc(o_done.next(), 1)

                    def values_copy(m, c):
                        dve.wait_ge(v_ps.sem, v_ps.count(m, c + 1))
                        nc.vector.tensor_copy(v[:, c, :, 0:HD], ps_v[0:CKEYS, :].rearrange("p (a b) -> p a b", b=HD)
                                              ).then_inc(v_done.next(), 1)

                    def chain(m, at):
                        def step(k, instruction):
                            instruction.then_inc(dg.next(), 1)
                            dve.wait_ge(dg.sem, dg.count(m, k))

                        i = (at - CH["stats"]) * STATS_PER_SLOT
                        if i == 0:
                            dve.wait_ge(x_in[m.parity()].sem, x_in[m.parity()].count(m, 16))
                            dve.wait_ge(dg.sem, dg.count(m, 0))
                        if 0 <= i < UNITS:
                            for u in range(i, min(i + STATS_PER_SLOT, UNITS)):
                                nc.vector.bn_stats(stats[:, u, :], raw[:, m.parity(), UPIX * u:UPIX * (u + 1)]
                                                   ).then_inc(bs_done.next(), 1)
                        if at == CH["aggr"]:
                            dve.wait_ge(bs_done.sem, bs_done.count(m, UNITS))
                            step(1, nc.vector.bn_aggr(st[:], stats[:].rearrange("p a b -> p (a b)")))
                        if at == CH["d1"]:
                            dve.wait_ge(cg.sem, cg.count(m, 1))
                            step(2, nc.vector.tensor_tensor(col(D), st[:, 0:1], ps_v[:, 0:1], ALU.subtract))
                            step(3, nc.vector.scalar_tensor_tensor(col(SQ), col(D), col(D), st[:, 1:2],
                                                                   ALU.mult, ALU.add))
                        if at == CH["d3"]:
                            dve.wait_ge(cg.sem, cg.count(m, 2))
                            step(4, nc.vector.tensor_scalar(col(VE), ps_v[:, 1:2], EPS, None, ALU.add))
                        if at == CH["d4"]:
                            dve.wait_ge(cg.sem, cg.count(m, 3))
                            step(5, nc.vector.tensor_tensor(col(POS, 3), ps_v[:, 4:7], base_f[:], ALU.add))
                            step(6, nc.vector.tensor_scalar(col(POS, 3), col(POS, 3), 0.0, P - 1.0, ALU.max, ALU.min))
                            step(7, nc.vector.tensor_copy(pooled_row[:], ps_v[:, 8:8 + P]))
                        if at == CH["d6"]:
                            dve.wait_ge(pg.sem, pg.count(m, 15))
                            step(8, nc.vector.scalar_tensor_tensor(junk[:], pooled_row[:], 1.0, hat_sum[:],
                                                                   ALU.mult, ALU.mult, accum_out=col(ZS)))
                        if at == CH["d7"]:
                            dve.wait_ge(ag.sem, ag.count(m, 4))
                            step(9, nc.vector.tensor_scalar(col(EX), col(EX), 1.0, None, ALU.add))
                            step(10, nc.vector.reciprocal(col(GATE), col(EX)))
                        if at == CH["d9"]:
                            dve.wait_ge(cg.sem, cg.count(m, 4))
                            step(11, nc.vector.tensor_tensor(col(D1), col(M1), ps_v[:, 2:3], ALU.subtract))
                            dve.wait_ge(pg.sem, pg.count(m, 23))
                            step(12, nc.vector.scalar_tensor_tensor(col(SQ1), col(D1), col(D1), col(AV),
                                                                    ALU.mult, ALU.add))
                        if at == CH["d11"]:
                            dve.wait_ge(cg.sem, cg.count(m, 5))
                            step(13, nc.vector.tensor_scalar(col(VE1), ps_v[:, 3:4], EPS, None, ALU.add))

                    def slot(n, t):
                        if n.exists():
                            masked(n, t)
                        m, k = lagged(n, t, NORM)
                        if k % TPG == 0 and m.exists():
                            normalised(m, k // TPG)
                        m, k = lagged(n, t, CT_COPY)
                        if k % TPG == 0 and m.exists():
                            context_copy(m, k // TPG)
                        m, k = lagged(n, t, FINAL)
                        if k % TPG == 0 and m.exists():
                            final(m, k // TPG)
                        for m, u, since in units_at(n, t):
                            if since == 6:
                                dve.wait_ge(kh_done.sem, kh_done.count(m, u + 1))
                                nc.vector.tensor_tensor(inside(kl, u, slice(0, HD)), halves(tqk[HD:P, :]),
                                                        inside(kh, u, slice(HD, P)).bitcast(F32),
                                                        ALU.subtract).then_inc(kl_done.next(), 1)
                            if since == 4:
                                dve.wait_ge(qk_done.sem, qk_done.count(m, u + 1))
                                tiles = query_tiles(u)
                                src = tqk[0:HD, :].rearrange("p (r s c) -> p r s c", s=STRIPS, c=SW)
                                nc.vector.tensor_copy(tiles[0:HD], src).then_inc(qh_done.next(), 1)
                                dve.wait_ge(qh_done.sem, qh_done.count(m, u + 1))
                                nc.vector.tensor_tensor(tiles[HD:P], src, tiles[0:HD].bitcast(F32),
                                                        ALU.subtract).then_inc(ql_done.next(), 1)
                                nc.vector.tensor_copy(inside(kh, u, slice(0, HD)), halves(tqk[HD:P, :])
                                                      ).then_inc(kh2_done.next(), 1)
                            if since == 5:
                                values_copy(m, u)
                            if since == 6 and u == UNITS - 1:
                                values_copy(m, u + 1)
                        for m, at in chain_at(n, t):
                            chain(m, at)

                    for n, t in slots(first, last, drain, register):
                        slot(n, t)

        def restart(rounds=1):
            for e in events:
                e.end_part(rounds)
            with nc.Block() as block:
                @block.gpsimd
                def _(gp):
                    gp.sem_clear(range(events[0].sem.num, events[-1].sem.num + 1))

        images(-2, 1)
        restart()
        with nc.Fori(0, ROUNDS) as i:
            images(2, 1 + ROUND, register=i)
            restart(ROUNDS)
        images(NIMG - 2, NIMG - 1, drain=DRAIN)


def kernel(**inputs):
    import numpy as _np
    import concourse.bacc as _bacc
    from concourse import mybir as _mybir
    from concourse.bass_utils import run_bass_kernel_spmd as _run

    a = {k.replace("L1_conv_", "").replace("L0_conv_", ""): _np.asarray(v) for k, v in inputs.items()}
    x = a["x"]

    def stacked(top, bottom, layer):
        return _np.stack([_np.concatenate([a[f"{top}{layer}_{p}"], a[f"{bottom}{layer}_{p}"]])
                          for p in ("b", "g", "be", "m", "v")], axis=1)
    arrays = {
        "x": x.reshape(NIMG, P, H * W),
        "par": _np.concatenate([stacked("q", "k", 1), stacked("q", "k", 2)], axis=1),
        "w1": _np.concatenate([a["q1_w"], a["k1_w"]], axis=0),
        "w2": _np.concatenate([a["q2_w"], a["k2_w"]], axis=0),
        "wv": _np.concatenate([a["v_w"], a["v_w"]], axis=0),
        "wo": _np.concatenate([a["w_w"], a["w_w"]], axis=1),
        "bo": a["w_b"].reshape(P, 1),
        "bv": _np.concatenate([a["v_b"], a["v_b"]]).reshape(P, 1),
        "wg": _np.concatenate([a["w_offset"].reshape(-1), a["w_deform"].reshape(-1), a["b_deform"].reshape(-1)]),
    }
    nc = _bacc.Bacc("TRN2", target_bir_lowering=False, num_devices=1)
    arrays = {f"in_{k}_dram": _np.ascontiguousarray(t) for k, t in arrays.items()}
    args = [nc.dram_tensor(k, t.shape, _mybir.dt.from_np(t.dtype), kind="ExternalInput").ap()
            for k, t in arrays.items()]
    args.append(nc.dram_tensor("out_0_dram", (NIMG, P, H * W), _mybir.dt.float32, kind="ExternalOutput").ap())
    build(nc, *args)
    r = _run(nc, [arrays], core_ids=[0])
    return r.results[0]["out_0_dram"].reshape(x.shape)
```
